# Optimizing a Trainium2 kernel written in Bass

```python
import numpy as np
import jax
import jax.numpy as jnp

def _softmax(x, axis=-1):
    return jax.nn.softmax(x, axis=axis)

def _gelu(x):
    return jax.nn.gelu(x, approximate=True)

def _silu(x):
    return jax.nn.silu(x)

def _sigmoid(x):
    return jax.nn.sigmoid(x)

def _layernorm(x, axis=-1, eps=1e-05):
    m = jnp.mean(x, axis=axis, keepdims=True)
    v = jnp.var(x, axis=axis, keepdims=True)
    return (x - m) / jnp.sqrt(v + eps)

def _scatter_add(tgt, idx, src, axis=0):
    return tgt.at[idx].add(src)

def _segment_sum(src, seg, n):
    return jax.ops.segment_sum(src, seg, n)
kernel_name = 'mk_adj_preln_d2_adj_r2_26a72e'

def setup_inputs(seed: int=0):
    np.random.seed(seed)
    _w = jnp.asarray

    def _rec_inputs():
        import jax
        import jax.numpy as jnp
        _gk = jax.random.key(seed)
        x = -0.000929 + 1 * jax.random.normal(jax.random.fold_in(_gk, 1), (8192, 128), jnp.float32)
        _a = jax.random.bernoulli(jax.random.fold_in(_gk, 2), 0.00195312, (8192, 8192))
        _a = jnp.logical_or(_a, jnp.swapaxes(_a, -1, -2))
        _a = jnp.logical_or(_a, jnp.eye(8192, dtype=bool))
        adj = _a.astype(jnp.int32)
        return (x, adj)
    x, adj = _rec_inputs()

    def _L0_gnn_setup():
        import jax, jax.numpy as jnp
        import numpy as np
        N = 4096
        IN = 128
        OUT = 128
        THR = 0.0001
        ALPHA = 0.2
        NEG = -1000000000.0
        key = jax.random.key(seed)
        k1, k2, k3, k4 = jax.random.split(key, 4)
        inp = jax.random.normal(k1, (N, IN), jnp.float32)
        W = jax.random.normal(k2, (IN, OUT), jnp.float32) * (1.414 * np.sqrt(2.0 / (IN + OUT)))
        a = jax.random.normal(k3, (2 * OUT, 1), jnp.float32) * (1.414 * np.sqrt(2.0 / (2 * OUT + 1)))
        adj = jax.random.randint(k4, (N, N), 0, 2, jnp.int32)
        return {'input': inp, 'W': W, 'a': a, 'adj': adj, 'M': N}
    _L0_gnn_all = _L0_gnn_setup()
    _L0_gnn_in = {k: v for k, v in _L0_gnn_all.items() if k in ('W', 'a')}
    del _L0_gnn_all

    def _L1_gnn_setup():
        import jax, jax.numpy as jnp
        import numpy as np
        ALPHA = 0.2
        NEG_INF = -9000000000000000.0
        key = jax.random.key(seed)
        k1, k2, k3, k4 = jax.random.split(key, 4)
        N, F_IN, F_OUT = (4096, 128, 128)
        h = jax.random.normal(k1, (N, F_IN), dtype=jnp.float32)
        adj = jax.random.randint(k2, (N, N), 0, 2, dtype=jnp.int32)
        W = jax.random.normal(k3, (F_IN, F_OUT), dtype=jnp.float32) * (1.414 / np.sqrt(F_IN))
        a = jax.random.normal(k4, (2 * F_OUT, 1), dtype=jnp.float32) * (1.414 / np.sqrt(2 * F_OUT))
        return {'h': h, 'adj': adj, 'W': W, 'a': a}
    _L1_gnn_all = _L1_gnn_setup()
    _L1_gnn_in = {k: v for k, v in _L1_gnn_all.items() if k in ('W', 'a')}
    del _L1_gnn_all
    return {'x': x, 'adj': adj, 'L0_gnn_W': _L0_gnn_in['W'], 'L0_gnn_a': _L0_gnn_in['a'], 'L1_gnn_W': _L1_gnn_in['W'], 'L1_gnn_a': _L1_gnn_in['a']}

def reference(x, adj, L0_gnn_W, L0_gnn_a, L1_gnn_W, L1_gnn_a):
    import jax
    import jax.numpy as jnp

    def _L0_gnn_ref(input, W, a, adj, M):
        import jax, jax.numpy as jnp
        import numpy as np
        N = 4096
        IN = 128
        OUT = 128
        THR = 0.0001
        ALPHA = 0.2
        NEG = -1000000000.0
        h = input @ W
        a_src = a[:OUT, 0]
        a_dst = a[OUT:, 0]
        e = jax.nn.leaky_relu((h[:M] @ a_src)[:, None] + (h @ a_dst)[None, :], negative_slope=ALPHA)
        valid = (adj[:M] > 0) & (h.sum(axis=1) != 0)[None, :]
        att = jax.nn.softmax(jnp.where(valid, e, NEG), axis=1)
        att = jnp.where(valid, att, 0.0)
        L = valid.sum(axis=1).astype(h.dtype)
        top = att.max(axis=1)
        attention = jnp.where(att >= THR, att, 0.0) * L[:, None]
        attention = jnp.where((top > THR)[:, None], attention, 0.0)
        h_prime = attention @ h
        return jax.nn.elu(h[:M] + h_prime)

    def _L1_gnn_ref(h, adj, W, a):
        import jax, jax.numpy as jnp
        import numpy as np
        ALPHA = 0.2
        NEG_INF = -9000000000000000.0
        Wh = h @ W
        F_out = W.shape[1]
        e_src = Wh @ a[:F_out, 0]
        e_dst = Wh @ a[F_out:, 0]
        e = jax.nn.leaky_relu(e_src[:, None] + e_dst[None, :], negative_slope=ALPHA)
        attention = jax.nn.softmax(jnp.where(adj > 0, e, NEG_INF), axis=1)
        h_prime = attention @ Wh
        return h_prime
    h = jnp.maximum(_layernorm(x, axis=-1), 0.0)
    x = x + _L0_gnn_ref(h, L0_gnn_W, L0_gnn_a, adj, 8192)
    h = jnp.maximum(_layernorm(x, axis=-1), 0.0)
    x = x + _L1_gnn_ref(h, adj, L1_gnn_W, L1_gnn_a)
    return x

_drawn_inputs = setup_inputs


def setup_inputs(seed=0):
    import zlib

    import numpy as np

    out = dict(_drawn_inputs(seed))
    spreads = {}
    factors = {'L1_gnn_a': 8.0}
    for name, (base, spread) in spreads.items():
        noise = np.random.default_rng([zlib.crc32(name.encode()), seed]).standard_normal(out[name].shape)
        drawn = base * np.exp(spread * noise) if base else spread * noise
        out[name] = jnp.asarray(drawn.astype(out[name].dtype))
    for name, factor in factors.items():
        out[name] = (out[name] * factor).astype(out[name].dtype)
    return out
```

```python
from contextlib import ExitStack

import concourse.bass as bass
from concourse import mybir

ALU = mybir.AluOpType
ACT = mybir.ActivationFunctionType
AX = mybir.AxisListType
F32 = mybir.dt.float32
I32 = mybir.dt.int32

N = 8192
F = 128
P = 128
T = N // P
FZ = F + 1
ALPHA = 0.2
THR = 1e-4
EPS = 1e-5

CH = 2048
NC = N // CH
SLOTS = 2
ADJS = 3
ACCS = 3
UJ = 8
U = T // UJ
UC = U // NC
Q = 16
QT = T // Q
QN = QT * P

UN = 6
LEAD = 4
LOOPS = (T - LEAD) // UN

DVE_UNITS = [[], [1, 5]]

FAST_SPREAD = 85.0
SHIFT = 30.0
MARGIN = 0.01
SMALL = 1e-30
NEVER = 1e30


def kernel_program(nc, x, adj, W0, a0, W1, a1, out):
    ctx = ExitStack()

    def sb(name, shape, dt=F32):
        return ctx.enter_context(nc.sbuf_tensor(name, shape, dt))

    def ps(name, cols):
        return ctx.enter_context(nc.psum_tensor(name, [P, cols], F32))

    sems = {}

    def sem(name):
        if name not in sems:
            sems[name] = ctx.enter_context(nc.semaphore(name))
        return sems[name]

    with ctx:
        d_row = sb("d_row", [P, N])
        row2 = sb("row2", [P, N])
        h_all = sb("h_all", [P, T, FZ])
        weights = [sb(f"weights{i}", [P, N]) for i in range(SLOTS)]
        adj_buf = [sb(f"adj_buf{i}", [P, CH], I32) for i in range(ADJS)]
        wT = [sb(f"wT{i}", [P, UJ * P]) for i in range(2)]
        ident = sb("ident", [P, P])
        ones = sb("ones", [P, P])
        minus_half = sb("minus_half", [P, 1])
        W_sb = sb("W_sb", [P, F])
        a_two = sb("a_two", [P, 2])
        a_dst_cols = sb("a_dst_cols", [P, P])
        mean_row = sb("mean_row", [P, F])
        h_sums = sb("h_sums", [P, Q])
        h_mean = sb("h_mean", [P, 1])
        sd_col = sb("sd_col", [P, T, 2])
        D_col = sb("D_col", [P, T])
        r_col = sb("r_col", [P, T])
        lin = sb("lin", [P, T])
        d_max = sb("d_max", [P, Q])
        d_min = sb("d_min", [P, Q])
        inv_any = sb("inv_any", [P, Q])
        top = sb("top", [P, 1])
        low = sb("low", [P, 1])
        base = sb("base", [P, 1])
        exp_bias = sb("exp_bias", [P, 3])
        flag = sb("flag", [P, 3])
        flag_i = sb("flag_i", [P, 1], I32)
        z_part = sb("z_part", [P, SLOTS, NC])
        cnt_part = sb("cnt_part", [P, SLOTS, NC])
        v_part = sb("v_part", [P, NC])
        v_top = sb("v_top", [P, 4])
        neg_m = sb("neg_m", [P, SLOTS])
        z_sum = sb("z_sum", [P, UN])
        n_edges = sb("n_edges", [P, UN])
        theta = sb("theta", [P, UN])
        scale = sb("scale", [P, UN])
        empty = sb("empty", [P, UN])
        x_res = sb("x_res", [P, ACCS, F])
        h_res = sb("h_res", [P, ACCS, F])
        y = sb("y", [P, F])
        y_exp = sb("y_exp", [P, F])
        rest = sb("rest", [P, F])
        x_out = sb("x_out", [P, ACCS, F])

        turn = [ps(f"turn{i}", UJ * P) for i in range(2)]
        acc = [ps(f"acc{i}", 512) for i in range(ACCS)]
        spare = ps("spare", 512)

        x_mid = nc.dram_tensor("x_mid", [N, F], F32, kind="Internal").ap()
        h_mid = nc.dram_tensor("h_mid", [N, F], F32, kind="Internal").ap()

        def constants():
            made = sem("constants_made")
            with nc.Block() as block:
                @block.gpsimd
                def _(pool):
                    nc.gpsimd.memset(ident[:], 0.0).then_inc(made, 1)
                    pool.wait_ge(made, 1)
                    nc.gpsimd.affine_select(out=ident[:], in_=ident[:], compare_op=ALU.not_equal, fill=1.0,
                                            base=0, pattern=[[-1, P]], channel_multiplier=1).then_inc(made, 1)

                @block.vector
                def _(dve):
                    nc.vector.memset(ones[:], 1.0)
                    nc.vector.memset(minus_half[:], -0.5)

        def prepare(layer, x_in, W_in, a_in):
            first = layer == 0
            x_all = weights[0][:].rearrange("p (t f) -> p t f", f=F)
            hn = weights[1][:].rearrange("p (t f) -> p t f", f=F)
            mean_diag = row2[:, 0:F]
            hnT = [row2[:, (1 + i) * QN:(2 + i) * QN] for i in range(2)]
            hT = [row2[:, (3 + i) * QN:(4 + i) * QN] for i in range(2)]
            inv = row2[:, 5 * QN:6 * QN]
            st = row2[:, 6 * QN:6 * QN + 6 * T].rearrange("p (t k) -> p t k", k=6)
            r0 = 8 * QN
            mean, var, rstd, tmp, tmp2 = [row2[:, r0 + i * T:r0 + (i + 1) * T] for i in range(5)]
            x_view = x_in.rearrange("(t p) f -> p t f", p=P)
            h_view = h_mid.rearrange("(t p) f -> p t f", p=P)
            h_stored = sem(f"p{layer}_h_stored")
            hn_ps = [turn[0][:, i * QN:(i + 1) * QN] for i in range(2)]
            h_ps = [turn[1][:, i * QN:(i + 1) * QN] for i in range(2)]
            hT_ps, d_ps, sum_ps, s_ps = acc[0], acc[1], acc[2], spare
            n = f"p{layer}_"
            x_loaded = [sem(n + f"x_loaded{i}") for i in range(4)]
            w_loaded = sem(n + "w_loaded")
            chain = sem(n + "vector_chain")
            a_cols = sem(n + "a_cols_ready")
            var_ready = sem(n + "var_ready")
            std_ready = sem(n + "std_ready")
            hn_ready = sem(n + "hn_ready")
            hn_turned = sem(n + "hn_turned")
            hnT_ready = sem(n + "hnT_ready")
            hT_done = sem(n + "hT_done")
            hT_ready = sem(n + "hT_ready")
            h_done = sem(n + "h_done")
            d_done = sem(n + "d_done")
            h_kept = sem(n + "h_kept")
            d_kept = sem(n + "d_kept")
            diag_ready = sem(n + "diag_ready")
            mean_done = sem(n + "mean_done")

            with nc.Block() as block:
                @block.sync
                def _(sp):
                    for i in range(4):
                        c = slice(i * T // 4, (i + 1) * T // 4)
                        sp.dma_start(x_all[:, c, :], x_view[:, c, :]).then_inc(x_loaded[i], 16)
                    sp.dma_start(W_sb[:], W_in).then_inc(w_loaded, 16)
                    sp.dma_start(a_two[:, 0:1], a_in[0:F, :]).then_inc(w_loaded, 16)
                    sp.dma_start(a_two[:, 1:2], a_in[F:2 * F, :]).then_inc(w_loaded, 16)
                    if first:
                        for q in range(Q):
                            sp.wait_ge(h_kept, q + 1)
                            sp.dma_start(h_view[:, q * QT:(q + 1) * QT, :], h_all[:, q * QT:(q + 1) * QT, 0:F])\
                                .then_inc(h_stored, 16)
                        sp.wait_ge(h_stored, 16 * Q)

                @block.vector
                def _(dve):
                    links = [0]

                    def link(ins):
                        links[0] += 1
                        ins.then_inc(chain, 1)
                        dve.wait_ge(chain, links[0])

                    for i in range(4):
                        dve.wait_ge(x_loaded[i], 16)
                        for t in range(i * T // 4, (i + 1) * T // 4):
                            last = nc.vector.bn_stats(st[:, t, :], x_all[:, t, :])
                    link(last)
                    link(nc.vector.tensor_tensor(mean, st[:, :, 1], st[:, :, 4], ALU.add))
                    link(nc.vector.tensor_scalar(mean, mean, 0.5, None, ALU.mult))
                    link(nc.vector.tensor_tensor(tmp, st[:, :, 1], st[:, :, 4], ALU.subtract))
                    link(nc.vector.tensor_tensor(tmp, tmp, tmp, ALU.mult))
                    link(nc.vector.tensor_tensor(var, st[:, :, 2], st[:, :, 5], ALU.add))
                    link(nc.vector.scalar_tensor_tensor(var, tmp, F / 4.0, var, ALU.mult, ALU.add))
                    nc.vector.tensor_scalar(var, var, 1.0 / F, EPS, ALU.mult, ALU.add).then_inc(var_ready, 1)
                    dve.wait_ge(std_ready, 1)
                    link(nc.vector.reciprocal(rstd, tmp2))
                    link(nc.vector.tensor_tensor(tmp, rstd, rstd, ALU.mult))
                    link(nc.vector.tensor_tensor(tmp, tmp, var, ALU.mult))
                    link(nc.vector.tensor_scalar(tmp, tmp, -0.5, 1.5, ALU.mult, ALU.add))
                    link(nc.vector.tensor_tensor(rstd, rstd, tmp, ALU.mult))
                    for t in range(T):
                        ins = nc.vector.tensor_scalar(hn[:, t, :], x_all[:, t, :], mean[:, t:t + 1], rstd[:, t:t + 1],
                                                      ALU.subtract, ALU.mult)
                        if t % QT == QT - 1:
                            ins.then_inc(hn_ready, 1)
                        if t == QT - 1:
                            dve.wait_ge(w_loaded, 48)
                            nc.vector.tensor_scalar(a_dst_cols[:], ones[:], a_two[:, 1:2], None, ALU.mult)\
                                .then_inc(a_cols, 1)
                    for q in range(Q):
                        cols = slice(q * QN, (q + 1) * QN)
                        dve.wait_ge(h_done, q + 1)
                        nc.vector.tensor_copy(h_all[:, q * QT:(q + 1) * QT, 0:F],
                                              h_ps[q % 2].rearrange("p (t f) -> p t f", f=F)).then_inc(h_kept, 1)
                        dve.wait_ge(d_done, q + 1)
                        nc.vector.tensor_reduce(d_max[:, q:q + 1], d_ps[:, 0:QN], AX.X, ALU.max)
                        nc.vector.tensor_reduce(d_min[:, q:q + 1], d_ps[:, 0:QN], AX.X, ALU.min)
                        if first:
                            link(nc.vector.tensor_scalar(inv, sum_ps[:, 0:QN], 0.0, None, ALU.is_equal, ALU.max,
                                                         accum_out=inv_any[:, q:q + 1]))
                            nc.vector.scalar_tensor_tensor(d_row[:, cols], inv, -NEVER, d_ps[:, 0:QN],
                                                           ALU.mult, ALU.add).then_inc(d_kept, 1)
                        else:
                            nc.vector.tensor_copy(d_row[:, cols], d_ps[:, 0:QN]).then_inc(d_kept, 1)
                    link(nc.vector.tensor_copy(sd_col[:], s_ps[:, 0:2 * T].rearrange("p (t k) -> p t k", k=2)))
                    link(nc.vector.tensor_reduce(top[:], d_max[:], AX.X, ALU.max))
                    link(nc.vector.tensor_reduce(low[:], d_min[:], AX.X, ALU.min))
                    link(nc.vector.tensor_scalar(base[:], low[:], -1.0, None, ALU.add))
                    link(nc.vector.tensor_scalar(exp_bias[:, 0:1], top[:], -1.0, SHIFT, ALU.mult, ALU.add))
                    link(nc.vector.tensor_scalar(exp_bias[:, 1:2], top[:], -ALPHA, SHIFT, ALU.mult, ALU.add))
                    link(nc.vector.tensor_scalar(exp_bias[:, 2:3], top[:], ALPHA - 1.0, None, ALU.mult))
                    link(nc.vector.tensor_scalar(lin[:], sd_col[:, :, 0], top[:, 0:1], 0.0, ALU.add, ALU.max))
                    link(nc.vector.tensor_tensor(flag[:, 0:1], top[:], low[:], ALU.subtract))
                    link(nc.vector.tensor_scalar(flag[:, 2:3], flag[:, 0:1], FAST_SPREAD, None, ALU.is_gt))
                    if first:
                        link(nc.vector.tensor_reduce(flag[:, 1:2], inv_any[:], AX.X, ALU.max))
                        link(nc.vector.tensor_tensor(flag[:, 2:3], flag[:, 2:3], flag[:, 1:2], ALU.max))
                    link(nc.vector.tensor_copy(flag_i[:], flag[:, 2:3]))
                    if not first:
                        dve.wait_ge(hT_ready, Q)
                        link(nc.vector.tensor_reduce(h_mean[:], h_sums[:], AX.X, ALU.add))
                        nc.vector.tensor_scalar(mean_diag, ident[:], h_mean[:, 0:1], 1.0 / N, ALU.mult, ALU.mult)\
                            .then_inc(diag_ready, 1)
                        dve.wait_ge(mean_done, 1)
                        nc.vector.tensor_copy(mean_row[:], hT_ps[:, 0:F])

                @block.scalar
                def _(act):
                    act.wait_ge(var_ready, 1)
                    nc.scalar.activation(tmp2, var, ACT.Sqrt).then_inc(std_ready, 1)
                    for q in range(Q):
                        act.wait_ge(hn_turned, q + 1)
                        if q >= 2:
                            act.wait_ge(h_done, q - 1)
                        nc.scalar.activation(hnT[q % 2], hn_ps[q % 2], ACT.Relu).then_inc(hnT_ready, 1)
                        act.wait_ge(hT_done, q + 1)
                        if q >= 2:
                            act.wait_ge(d_done, q - 1)
                        nc.scalar.activation(hT[q % 2], hT_ps[:, 0:QN], ACT.Identity,
                                             accum_out=h_sums[:, q:q + 1]).then_inc(hT_ready, 1)

                @block.tensor
                def _(pe):
                    def turn_hn(q):
                        pe.wait_ge(hn_ready, q + 1)
                        if q >= 2:
                            pe.wait_ge(hnT_ready, q - 1)
                        for i in range(QT):
                            last = nc.tensor.transpose(hn_ps[q % 2][:, i * P:(i + 1) * P], hn[:, q * QT + i, :], ident[:])
                        last.then_inc(hn_turned, 1)

                    def products(q):
                        pe.wait_ge(hnT_ready, q + 1)
                        if q >= 1:
                            pe.wait_ge(hT_ready, q)
                        nc.tensor.matmul(hT_ps[:, 0:QN], W_sb[:], hnT[q % 2], start=True, stop=True).then_inc(hT_done, 1)
                        if q >= 2:
                            pe.wait_ge(h_kept, q - 1)
                        for i in range(QT):
                            last = nc.tensor.matmul(h_ps[q % 2][:, i * F:(i + 1) * F], hnT[q % 2][:, i * P:(i + 1) * P],
                                                    W_sb[:], start=True, stop=True)
                        last.then_inc(h_done, 1)

                    def scores(q):
                        pe.wait_ge(hT_ready, q + 1)
                        if q >= 1:
                            pe.wait_ge(d_kept, q)
                        if q == 0:
                            pe.wait_ge(a_cols, 1)
                        nc.tensor.matmul(d_ps[:, 0:QN], a_dst_cols[:], hT[q % 2], start=True, stop=True)
                        if first:
                            nc.tensor.matmul(sum_ps[:, 0:QN], ones[:], hT[q % 2], start=True, stop=True)
                        for i in range(QT):
                            t = q * QT + i
                            last = nc.tensor.matmul(s_ps[:, 2 * t:2 * t + 2], hT[q % 2][:, i * P:(i + 1) * P], a_two[:],
                                                    start=True, stop=True)
                        last.then_inc(d_done, 1)

                    turn_hn(0)
                    pe.wait_ge(w_loaded, 48)
                    for q in range(Q):
                        if q + 1 < Q:
                            turn_hn(q + 1)
                        products(q)
                        if q >= 1:
                            scores(q - 1)
                    scores(Q - 1)
                    if not first:
                        pe.wait_ge(diag_ready, 1)
                        nc.tensor.matmul(hT_ps[:, 0:F], ones[:], mean_diag, start=True, stop=True)\
                            .then_inc(mean_done, 1)

        def attend(layer, general, x_in, x_to):
            first = layer == 0
            n = f"a{layer}_"
            folded = not first and not general
            LK = 2 * NC if general else NC
            COLS = FZ if folded else F
            adj_loaded = [sem(n + f"adj_loaded{i}") for i in range(ADJS)]
            row_link = sem(n + "row_link")
            row_done = sem(n + "row_functions_done")
            adj_used = sem(n + "adj_used")
            adj_counted = sem(n + "adj_counted")
            probe_link = sem(n + "probe_link")
            probed = sem(n + "chunk_probed")
            m_ready = sem(n + "m_ready")
            lrelu_link = sem(n + "lrelu_link")
            lrelu_done = sem(n + "lrelu_done")
            e_ready = sem(n + "e_ready")
            formed = sem(n + "factored_formed")
            thresholded = sem(n + "thresholded")
            turned = sem(n + "unit_turned")
            by_act = sem(n + "wT_by_act")
            by_dve = sem(n + "wT_by_dve")
            summed = sem(n + "unit_summed")
            acc_read = sem(n + "acc_read")
            y_neg_ready = sem(n + "y_neg_ready")
            y_exp_ready = sem(n + "y_exp_ready")
            rest_link = sem(n + "rest_link")
            res_loaded = [sem(n + f"res_loaded{i}") for i in range(ACCS)]
            out_ready = sem(n + "out_ready")
            stored = [sem(n + f"stored{i}") for i in range(ACCS)]
            tile_link = sem(n + "tile_link")
            finish_link = sem(n + "finish_link")
            SHIFT_LINKS = 4 if general else 0
            TILE_LINKS = SHIFT_LINKS + (3 if first else 1)
            FINISH_LINKS = 3
            RES = 32 if first else 16

            dve_units = [] if general else DVE_UNITS[layer]
            act_units = [u for u in range(U) if u not in dve_units]

            x_view = x_in.rearrange("(t p) f -> t p f", p=P)
            h_view = h_mid.rearrange("(t p) f -> t p f", p=P)
            out_view = x_to.rearrange("(t p) f -> t p f", p=P)
            adj_view = adj.rearrange("(t p) (c n) -> t p c n", p=P, n=CH)

            def chunk(c):
                return slice(c * CH, (c + 1) * CH)

            def steps(eng, step):
                for st in range(LEAD):
                    step(0, st)
                with eng.Fori(0, LOOPS) as it:
                    for r in range(UN):
                        step(it, LEAD + r)
                for st in range(LEAD + LOOPS * UN, T + 3):
                    step(0, st)

            def wait(eng, sm, it, per_step, value):
                if value > 0:
                    eng.wait_ge(sm, it * (UN * per_step) + value)

            def runs(st, lag):
                return 0 <= st - lag < T

            def wait_adj(eng, it, st, i):
                no = st * LK + i
                eng.wait_ge(adj_loaded[no % ADJS], it * (UN * LK // ADJS * 16) + (no // ADJS + 1) * 16)

            def wait_slot(eng, it, st, c):
                wait(eng, turned, it, U, (st - SLOTS) * U + (c + 1) * UC if st >= SLOTS else 0)

            def wait_moved(eng, it, st, u):
                if u < 0:
                    st, u = st - 1, u + U
                if u in dve_units:
                    wait(eng, by_dve, it, len(dve_units),
                         (st - 1) * len(dve_units) + dve_units.index(u) + 1 if st >= 1 else 0)
                else:
                    wait(eng, by_act, it, len(act_units),
                         (st - 1) * len(act_units) + act_units.index(u) + 1 if st >= 1 else 0)

            def sync_rows(sp):
                def step(it, st):
                    for i in range(LK):
                        if runs(st, 0):
                            no = st * LK + i
                            wait(sp, adj_used, it, LK, no - ADJS + 1)
                            if first and not general:
                                wait(sp, adj_counted, it, LK, no - ADJS + 1)
                            sp.dma_start(adj_buf[no % ADJS][:], adj_view[it * UN + st, :, i % NC, :])\
                                .then_inc(adj_loaded[no % ADJS], 16)
                        if i == 2 and runs(st, 3):
                            b = (st - 3) % ACCS
                            wait(sp, out_ready, it, 1, st - 2)
                            sp.dma_start(out_view[it * UN + (st - 3)], x_out[:, b]).then_inc(stored[b], 16)
                        if i == 3 and runs(st, 1):
                            b = (st - 1) % ACCS
                            wait(sp, out_ready, it, 1, st - ACCS)
                            sp.dma_start(x_res[:, b], x_view[it * UN + (st - 1)]).then_inc(res_loaded[b], 16)
                            if first:
                                sp.dma_start(h_res[:, b], h_view[it * UN + (st - 1)]).then_inc(res_loaded[b], 16)

                steps(sp, step)
                for b in range(ACCS):
                    sp.wait_ge(stored[b], 16 * len(range(b, T, ACCS)))

            def scalar_rows(act):
                def move_unit(it, st, u):
                    if runs(st, 1) and u in act_units:
                        wait(act, turned, it, U, (st - 1) * U + u + 1)
                        wait(act, summed, it, U, (st - 1) * U + u - 1)
                        nc.scalar.activation(wT[u % 2][:], turn[u % 2][:], ACT.Relu if folded else ACT.Identity)\
                            .then_inc(by_act, 1)

                def count(it, st, c):
                    wait_adj(act, it, st, c)
                    wait_slot(act, it, st, c)
                    if c == 0:
                        wait(act, m_ready, it, 1, st - SLOTS + 1)
                    no = st * LK + c
                    nc.scalar.activation(weights[st % SLOTS][:, chunk(c)], adj_buf[no % ADJS][:], ACT.Sign,
                                         bias=minus_half[:, 0:1], accum_out=cnt_part[:, st % SLOTS, c:c + 1])\
                        .then_inc(adj_counted, 1)

                def step(it, st):
                    for c in range(NC):
                        if first and not general and runs(st, 0):
                            count(it, st, c)
                        for u in range(c * UC, (c + 1) * UC):
                            move_unit(it, st, u)
                        if first and c == 1 and runs(st, 2):
                            wait(act, acc_read, it, 1, st - 1)
                            wait(act, rest_link, it, 2, (st - 3) * 2 + 1)
                            nc.scalar.activation(y_exp[:], y[:], ACT.Relu, scale=-1.0).then_inc(y_neg_ready, 1)
                            wait(act, y_neg_ready, it, 1, st - 1)
                            nc.scalar.activation(y_exp[:], y_exp[:], ACT.Exp, scale=-1.0).then_inc(y_exp_ready, 1)
                    if general and runs(st, 0):
                        wait(act, m_ready, it, 1, st + 1)
                        for c in range(NC):
                            w = weights[st % SLOTS][:, chunk(c)]
                            wait(act, lrelu_done, it, NC, st * NC + c + 1)
                            nc.scalar.activation(w, w, ACT.Exp, bias=neg_m[:, st % SLOTS:st % SLOTS + 1])\
                                .then_inc(e_ready, 1)

                if not general:
                    row = weights[0] if first else row2
                    nc.scalar.activation(r_col[:], lin[:], ACT.Exp, scale=ALPHA - 1.0)
                    if first:
                        nc.scalar.activation(row2[:], d_row[:], ACT.Exp, scale=ALPHA, bias=exp_bias[:, 1:2])\
                            .then_inc(row_link, 1)
                        act.wait_ge(row_link, 1)
                        nc.scalar.activation(d_row[:], d_row[:], ACT.Exp, bias=exp_bias[:, 0:1])\
                            .then_inc(row_done, 1)
                    else:
                        nc.scalar.activation(D_col[:], sd_col[:, :, 1], ACT.Exp, scale=ALPHA,
                                             bias=exp_bias[:, 1:2]).then_inc(row_link, 1)
                        nc.scalar.activation(d_row[:], d_row[:], ACT.Exp, scale=1.0 - ALPHA,
                                             bias=exp_bias[:, 2:3]).then_inc(row_done, 1)
                steps(act, step)

            def tensor_rows(pe):
                def turn_unit(it, st, u):
                    if u % UC == 0:
                        c = u // UC
                        if first:
                            wait(pe, thresholded, it, NC, (st - 1) * NC + c + 1)
                        else:
                            wait(pe, adj_used, it, LK, (st - 1) * LK + LK - NC + c + 1)
                    wait_moved(pe, it, st, u - 2)
                    for b in range(UJ):
                        j = (u * UJ + b) * P
                        last = nc.tensor.transpose(turn[u % 2][:, b * P:(b + 1) * P],
                                                   weights[(st - 1) % SLOTS][:, j:j + P], ident[:])
                    last.then_inc(turned, 1)

                def sum_unit(it, st, u):
                    wait_moved(pe, it, st, u)
                    if u == 0:
                        wait(pe, acc_read, it, 1, st - ACCS)
                    for b in range(UJ):
                        j = u * UJ + b
                        last = nc.tensor.matmul(acc[(st - 1) % ACCS][:, 0:COLS], wT[u % 2][:, b * P:(b + 1) * P],
                                                h_all[:, j, 0:COLS], start=(j == 0), stop=(j == T - 1))
                    last.then_inc(summed, 1)

                def step(it, st):
                    if runs(st, 1):
                        for u in range(U + 1):
                            if u < U:
                                turn_unit(it, st, u)
                            if u >= 1:
                                sum_unit(it, st, u - 1)

                if folded:
                    pe.wait_ge(row_link, 3)
                steps(pe, step)

            def vector_rows(dve):
                def link(ins, sm, it, per_step, value):
                    ins.then_inc(sm, 1)
                    wait(dve, sm, it, per_step, value)

                def tlink(ins, it, st, i):
                    link(ins, tile_link, it, TILE_LINKS, st * TILE_LINKS + i)

                def flink(ins, it, st, i):
                    link(ins, finish_link, it, FINISH_LINKS, (st - 2) * FINISH_LINKS + i)

                def move_unit(it, st, u):
                    if runs(st, 1) and u in dve_units:
                        wait(dve, turned, it, U, (st - 1) * U + u + 1)
                        wait(dve, summed, it, U, (st - 1) * U + u - 1)
                        if folded:
                            nc.vector.tensor_scalar(wT[u % 2][:], turn[u % 2][:], 0.0, None, ALU.max)\
                                .then_inc(by_dve, 1)
                        else:
                            nc.vector.tensor_copy(wT[u % 2][:], turn[u % 2][:]).then_inc(by_dve, 1)

                def row_scalar(cols, it, st):
                    return cols[:, bass.ds(it * UN + st, 1)]

                def probe(it, st, c):
                    w = weights[st % SLOTS][:, chunk(c)]
                    wait_adj(dve, it, st, c)
                    wait_slot(dve, it, st, c)
                    nc.vector.scalar_tensor_tensor(w, adj_buf[(st * LK + c) % ADJS][:], 0.0, row2[:, chunk(c)],
                                                   ALU.is_gt, ALU.mult).then_inc(adj_used, 1)
                    wait(dve, adj_used, it, LK, st * LK + c + 1)
                    nc.vector.tensor_reduce(v_part[:, c:c + 1], w, AX.X, ALU.max).then_inc(probe_link, 1)
                    wait(dve, probe_link, it, NC, st * NC + c + 1)
                    nc.vector.tensor_scalar(w, w, 0.0, None, ALU.is_gt, ALU.add,
                                            accum_out=cnt_part[:, st % SLOTS, c:c + 1]).then_inc(probed, 1)

                def shift(it, st):
                    wait(dve, probed, it, NC, (st + 1) * NC)
                    tlink(nc.vector.tensor_reduce(v_top[:, 0:1], v_part[:], AX.X, ALU.max), it, st, 1)
                    tlink(nc.vector.tensor_scalar(v_top[:, 1:2], v_top[:, 0:1], base[:, 0:1], None, ALU.add),
                          it, st, 2)
                    tlink(nc.vector.tensor_tensor(v_top[:, 2:3], v_top[:, 1:2],
                                                  sd_col[:, bass.ds(it * UN + st, 1), 0], ALU.add), it, st, 3)
                    tlink(nc.vector.scalar_tensor_tensor(v_top[:, 3:4], v_top[:, 2:3], ALPHA, v_top[:, 2:3],
                                                         ALU.mult, ALU.max), it, st, 4)
                    nc.vector.tensor_scalar(neg_m[:, st % SLOTS:st % SLOTS + 1], v_top[:, 3:4], -1.0, -MARGIN,
                                            ALU.mult, ALU.add).then_inc(m_ready, 1)

                def lrelu(it, st, c):
                    w = weights[st % SLOTS][:, chunk(c)]
                    nc.vector.tensor_scalar(w, d_row[:, chunk(c)], sd_col[:, bass.ds(it * UN + st, 1), 0], None,
                                            ALU.add).then_inc(lrelu_link, 1)
                    wait(dve, lrelu_link, it, NC, st * NC + c + 1)
                    nc.vector.scalar_tensor_tensor(w, w, ALPHA, w, ALU.mult, ALU.max).then_inc(lrelu_done, 1)

                def mask_general(it, st, c):
                    w = weights[st % SLOTS][:, chunk(c)]
                    wait_adj(dve, it, st, NC + c)
                    wait(dve, e_ready, it, NC, st * NC + c + 1)
                    nc.vector.scalar_tensor_tensor(w, adj_buf[(st * LK + NC + c) % ADJS][:], 0.0, w, ALU.max, ALU.min,
                                                   accum_out=z_part[:, st % SLOTS, c:c + 1]).then_inc(adj_used, 1)

                def form(it, st, c):
                    w = weights[st % SLOTS][:, chunk(c)]
                    wait_slot(dve, it, st, c)
                    wait(dve, adj_counted, it, NC, st * NC + c + 1)
                    nc.vector.scalar_tensor_tensor(w, row2[:, chunk(c)], row_scalar(r_col, it, st),
                                                   d_row[:, chunk(c)], ALU.mult, ALU.max).then_inc(formed, 1)

                def mask(it, st, c):
                    w = weights[st % SLOTS][:, chunk(c)]
                    wait(dve, formed, it, NC, st * NC + c + 1)
                    nc.vector.scalar_tensor_tensor(w, adj_buf[(st * LK + c) % ADJS][:], 0.0, w, ALU.is_gt, ALU.mult,
                                                   accum_out=z_part[:, st % SLOTS, c:c + 1]).then_inc(adj_used, 1)

                def form_masked(it, st, c):
                    wait_adj(dve, it, st, c)
                    wait_slot(dve, it, st, c)
                    nc.vector.scalar_tensor_tensor(weights[st % SLOTS][:, chunk(c)], d_row[:, chunk(c)],
                                                   row_scalar(r_col, it, st), adj_buf[(st * LK + c) % ADJS][:],
                                                   ALU.max, ALU.min).then_inc(adj_used, 1)

                def row_sums(it, st):
                    b = slice(st % UN, st % UN + 1)
                    wait(dve, adj_used, it, LK, (st + 1) * LK)
                    if first:
                        tlink(nc.vector.tensor_reduce(n_edges[:, b], cnt_part[:, st % SLOTS, :], AX.X, ALU.add),
                              it, st, SHIFT_LINKS + 1)
                        if not general:
                            nc.vector.tensor_scalar(n_edges[:, b], n_edges[:, b], 0.5, N / 2.0, ALU.mult, ALU.add)\
                                .then_inc(m_ready, 1)
                    ins = nc.vector.tensor_reduce(z_sum[:, b], z_part[:, st % SLOTS, :], AX.X, ALU.add)
                    if first:
                        tlink(ins, it, st, SHIFT_LINKS + 2)
                        tlink(nc.vector.tensor_scalar(theta[:, b], z_sum[:, b], THR, None, ALU.mult),
                              it, st, SHIFT_LINKS + 3)
                    else:
                        tlink(ins, it, st, SHIFT_LINKS + 1)

                def threshold(it, st, c):
                    w = weights[st % SLOTS][:, chunk(c)]
                    nc.vector.scalar_tensor_tensor(w, w, theta[:, st % UN:st % UN + 1], w, ALU.is_ge, ALU.mult)\
                        .then_inc(thresholded, 1)

                def finish(it, st):
                    g = st - 2
                    a = acc[g % ACCS]
                    b = slice(g % UN, g % UN + 1)
                    z = a[:, F:FZ] if folded else z_sum[:, b]
                    wait(dve, summed, it, U, (g + 1) * U)
                    flink(nc.vector.tensor_scalar(scale[:, b], z, SMALL, None, ALU.max), it, st, 1)
                    flink(nc.vector.reciprocal(scale[:, b], scale[:, b]), it, st, 2)
                    no = g // ACCS
                    wait(dve, res_loaded[g % ACCS], it, 0, 0)
                    dve.wait_ge(res_loaded[g % ACCS], it * (UN // ACCS * RES) + (no + 1) * RES)
                    if first:
                        flink(nc.vector.tensor_tensor(scale[:, b], scale[:, b], n_edges[:, b], ALU.mult), it, st, 3)
                        wait(dve, y_exp_ready, it, 1, g)
                        nc.vector.scalar_tensor_tensor(y[:], a[:, 0:F], scale[:, b], h_res[:, g % ACCS],
                                                       ALU.mult, ALU.add).then_inc(acc_read, 1)
                        return
                    if no >= 1:
                        dve.wait_ge(stored[g % ACCS], it * (UN // ACCS * 16) + no * 16)
                    flink(nc.vector.tensor_scalar(empty[:, b], z, 0.0, None, ALU.is_le), it, st, 3)
                    nc.vector.scalar_tensor_tensor(x_out[:, g % ACCS], a[:, 0:F], scale[:, b], x_res[:, g % ACCS],
                                                   ALU.mult, ALU.add).then_inc(acc_read, 1)
                    wait(dve, acc_read, it, 1, g + 1)
                    nc.vector.scalar_tensor_tensor(x_out[:, g % ACCS], mean_row[:], empty[:, b], x_out[:, g % ACCS],
                                                   ALU.mult, ALU.add).then_inc(out_ready, 1)

                def finish_elu(it, st):
                    g = st - 2
                    wait(dve, y_exp_ready, it, 1, g + 1)
                    link(nc.vector.tensor_scalar(rest[:], y_exp[:], -1.0, None, ALU.add),
                         rest_link, it, 2, g * 2 + 1)
                    if g >= ACCS:
                        dve.wait_ge(stored[g % ACCS], it * (UN // ACCS * 16) + g // ACCS * 16)
                    link(nc.vector.scalar_tensor_tensor(rest[:], y[:], 0.0, rest[:], ALU.max, ALU.add),
                         rest_link, it, 2, g * 2 + 2)
                    nc.vector.tensor_tensor(x_out[:, g % ACCS], rest[:], x_res[:, g % ACCS], ALU.add)                        .then_inc(out_ready, 1)

                def step(it, st):
                    makes, finishes = runs(st, 0), runs(st, 2)
                    if general:
                        if makes:
                            for c in range(NC):
                                probe(it, st, c)
                            shift(it, st)
                            for c in range(NC):
                                lrelu(it, st, c)
                            for c in range(NC):
                                mask_general(it, st, c)
                            row_sums(it, st)
                            if first:
                                for c in range(NC):
                                    threshold(it, st, c)
                        if finishes:
                            finish(it, st)
                            if first:
                                finish_elu(it, st)
                        return
                    if makes and first:
                        form(it, st, 0)
                    for c in range(NC):
                        if makes and first:
                            if c + 1 < NC:
                                form(it, st, c + 1)
                            mask(it, st, c)
                        elif makes:
                            form_masked(it, st, c)
                        for u in range(c * UC, (c + 1) * UC):
                            move_unit(it, st, u)
                        if c == 0 and finishes:
                            finish(it, st)
                    if makes and first:
                        row_sums(it, st)
                        for c in range(NC):
                            threshold(it, st, c)
                    if first and finishes:
                        finish_elu(it, st)

                if general:
                    nc.vector.tensor_scalar(row2[:], d_row[:], base[:, 0:1], 0.0, ALU.subtract, ALU.max)\
                        .then_inc(row_link, 1)
                    dve.wait_ge(row_link, 1)
                elif first:
                    dve.wait_ge(row_done, 1)
                else:
                    dve.wait_ge(row_link, 1)
                    D = D_col[:].rearrange("p (t o) -> p t o", o=1)
                    nc.vector.tensor_tensor(h_all[:, :, 0:F], h_all[:, :, 0:F], D.to_broadcast([P, T, F]), ALU.mult)\
                        .then_inc(row_link, 1)
                    nc.vector.tensor_copy(h_all[:, :, F:FZ], D).then_inc(row_link, 1)
                    dve.wait_ge(row_done, 1)
                steps(dve, step)

            return sync_rows, scalar_rows, tensor_rows, vector_rows

        constants()
        for layer, x_in, W_in, a_in, x_to in ((0, x, W0, a0, x_mid), (1, x_mid, W1, a1, out)):
            prepare(layer, x_in, W_in, a_in)
            general = attend(layer, True, x_in, x_to)
            fast = attend(layer, False, x_in, x_to)

            def flagged(eng, which):
                wide = eng.value_load(flag_i[0:1, 0:1], min_val=0, max_val=1)
                with eng.If(wide > 0):
                    general[which](eng)
                with eng.Else():
                    fast[which](eng)

            with nc.Block() as block:
                @block.sync
                def _(sp):
                    flagged(sp, 0)

                @block.scalar
                def _(act):
                    flagged(act, 1)

                @block.tensor
                def _(pe):
                    flagged(pe, 2)

                @block.vector
                def _(dve):
                    flagged(dve, 3)


_INS = ['x', 'adj', 'L0_gnn_W', 'L0_gnn_a', 'L1_gnn_W', 'L1_gnn_a']
_OUTS = [((8192, 128), 'float32')]


def kernel(**inputs):
    import numpy as _np
    import concourse.bacc as _bacc
    from concourse import mybir as _mybir
    from concourse.bass_utils import run_bass_kernel_spmd as _run

    nc = _bacc.Bacc("TRN2", target_bir_lowering=False, num_devices=1)
    arrays, args = {}, []
    for name in _INS:
        a = _np.ascontiguousarray(inputs[name])
        arrays[f"in_{name}_dram"] = a
        args.append(nc.dram_tensor(f"in_{name}_dram", a.shape, _mybir.dt.from_np(a.dtype), kind="ExternalInput").ap())
    for i, (shape, dtype) in enumerate(_OUTS):
        dt = _mybir.dt.from_np(_np.dtype(dtype))
        args.append(nc.dram_tensor(f"out_{i}_dram", shape, dt, kind="ExternalOutput").ap())
    kernel_program(nc, *args)
    r = _run(nc, [arrays], core_ids=[0])
    got = tuple(r.results[0][f"out_{i}_dram"] for i in range(len(_OUTS)))
    return got[0]
```

```python
from contextlib import ExitStack

import concourse.bass as bass
from concourse import mybir

ALU = mybir.AluOpType
ACT = mybir.ActivationFunctionType
AX = mybir.AxisListType
F32 = mybir.dt.float32
BF16 = mybir.dt.bfloat16
U8 = mybir.dt.uint8
I32 = mybir.dt.int32

N = 8192
F = 128
P = 128
T = N // P
FZ = F + 1
ALPHA = 0.2
THR = 1e-4
EPS = 1e-5

CH = 2048
NC = N // CH
SLOTS = 2
ADJS = 3
ACCS = 3
UJ = 8
U = T // UJ
UC = U // NC
Q = 16
QT = T // Q
QN = QT * P

UN = 6
LEAD = 4
LOOPS = (T - LEAD) // UN

G0 = 4
GI = G0 * P
NG = T // G0
G1 = 8
CB = CH // P
PAIRS = T // 2
RING = 4
CP = PAIRS // NC

FAST_SPREAD = 85.0
SHIFT = 30.0
MARGIN = 0.01
SMALL = 1e-30
NEVER = 1e30


def kernel_program(nc, x, adj, W0, a0, W1, a1, out):
    ctx = ExitStack()

    def sb(name, shape, dt=F32):
        return ctx.enter_context(nc.sbuf_tensor(name, shape, dt))

    def ps(name, cols):
        return ctx.enter_context(nc.psum_tensor(name, [P, cols], F32))

    sems = {}

    def sem(name):
        if name not in sems:
            sems[name] = ctx.enter_context(nc.semaphore(name))
        return sems[name]

    with ctx:
        arena = sb("arena", [P, 5 * N])

        def part(start, size):
            return arena[:, start:start + size]

        d_row = part(0, N)
        s_row = part(N, N)
        row2 = s_row
        weights = [part((2 + i) * N, N) for i in range(SLOTS)]
        adj_buf = [part(4 * N + i * CH, CH).bitcast(I32) for i in range(ADJS)]
        wT = [part(4 * N + ADJS * CH + i * UJ * P, UJ * P) for i in range(2)]
        h_all = sb("h_all", [P, T, FZ])
        identb = sb("identb", [P, P], BF16)
        ident = sb("ident", [P, P])
        ones = sb("ones", [P, P])
        W_sb = sb("W_sb", [P, F])
        a_two = sb("a_two", [P, 2])
        a_dst_cols = sb("a_dst_cols", [P, P])
        a_src_cols = sb("a_src_cols", [P, P])
        mean_row = sb("mean_row", [P, F])
        h_sums = sb("h_sums", [P, Q])
        h_mean = sb("h_mean", [P, 1])
        sd_col = sb("sd_col", [P, T, 2])
        D_col = sb("D_col", [P, T])
        rho_col = sb("rho_col", [P, T])
        r_col = sb("r_col", [P, T])
        low_exp = sb("low_exp", [P, 2])
        at_risk = sb("at_risk", [P, T])
        path = sb("path", [P, 2], I32)
        path_f = sb("path_f", [P, 2])
        lin = sb("lin", [P, T])
        d_max = sb("d_max", [P, Q])
        d_min = sb("d_min", [P, Q])
        inv_any = sb("inv_any", [P, Q])
        top = sb("top", [P, 1])
        low = sb("low", [P, 1])
        base = sb("base", [P, 1])
        exp_bias = sb("exp_bias", [P, 3])
        flag = sb("flag", [P, 3])
        edges_kept = sb("edges_kept", [P, 1])
        z_part = sb("z_part", [P, SLOTS, NC])
        cnt_part = sb("cnt_part", [P, SLOTS, NC])
        v_part = sb("v_part", [P, NC])
        v_top = sb("v_top", [P, 4])
        neg_m = sb("neg_m", [P, SLOTS])
        z_sum = sb("z_sum", [P, UN])
        n_edges = sb("n_edges", [P, UN])
        theta = sb("theta", [P, UN])
        scale = sb("scale", [P, UN])
        empty = sb("empty", [P, UN])
        x_res = sb("x_res", [P, ACCS, F])
        h_res = sb("h_res", [P, ACCS, F])
        y = sb("y", [P, F])
        y_exp = sb("y_exp", [P, F])
        rest = sb("rest", [P, F])
        x_out = sb("x_out", [P, ACCS, F])

        psum = ps("psum", 8 * 512)

        def bank(i, banks=1):
            return psum[:, i * 512:(i + banks) * 512]

        turn = [bank(0, 2), bank(2, 2)]
        acc = [bank(4 + i) for i in range(ACCS)]
        spare = bank(7)

        x_mid = nc.dram_tensor("x_mid", [N, F], F32, kind="Internal").ap()
        h_mid = nc.dram_tensor("h_mid", [N, F], F32, kind="Internal").ap()
        d_mid = nc.dram_tensor("d_mid", [1, N], F32, kind="Internal").ap()
        edgesT = nc.dram_tensor("edgesT", [NG * NC, P, CB * GI], U8, kind="Internal").ap()

        def constants():
            made = sem("constants_made")
            with nc.Block() as block:
                @block.gpsimd
                def _(pool):
                    nc.gpsimd.memset(ident[:], 0.0).then_inc(made, 1)
                    pool.wait_ge(made, 1)
                    nc.gpsimd.affine_select(out=ident[:], in_=ident[:], compare_op=ALU.not_equal, fill=1.0,
                                            base=0, pattern=[[-1, P]], channel_multiplier=1).then_inc(made, 1)
                    pool.wait_ge(made, 2)
                    nc.gpsimd.tensor_copy(identb[:], ident[:])

                @block.vector
                def _(dve):
                    nc.vector.memset(ones[:], 1.0)

        def prepare(layer, x_in, W_in, a_in):
            first = layer == 0
            x_all = weights[0].rearrange("p (t f) -> p t f", f=F)
            hn = weights[1].rearrange("p (t f) -> p t f", f=F)
            work = 4 * N
            mean_diag = part(work, F)
            hnT = [part(work + (1 + i) * QN, QN) for i in range(2)]
            hT = [part(work + (3 + i) * QN, QN) for i in range(2)]
            inv = part(work + 5 * QN, QN)
            st = part(work + 6 * QN, 6 * T).rearrange("p (t k) -> p t k", k=6)
            mean, var, rstd, tmp, tmp2 = [part(work + 8 * QN + i * T, T) for i in range(5)]
            x_view = x_in.rearrange("(t p) f -> p t f", p=P)
            h_view = h_mid.rearrange("(t p) f -> p t f", p=P)
            h_stored = sem(f"p{layer}_h_stored")
            hn_ps = [turn[0][:, i * QN:(i + 1) * QN] for i in range(2)]
            h_ps = turn[1][:, 0:QN]
            sr_ps = turn[1][:, QN:2 * QN]
            s_kept = sem(f"p{layer}_s_kept")
            hT_ps, d_ps, sum_ps, s_ps = acc[0], acc[1], acc[2], spare
            n = f"p{layer}_"
            x_loaded = [sem(n + f"x_loaded{i}") for i in range(4)]
            w_loaded = sem(n + "w_loaded")
            chain = sem(n + "vector_chain")
            a_cols = sem(n + "a_cols_ready")
            var_ready = sem(n + "var_ready")
            std_ready = sem(n + "std_ready")
            hn_ready = sem(n + "hn_ready")
            hn_turned = sem(n + "hn_turned")
            hnT_ready = sem(n + "hnT_ready")
            hT_done = sem(n + "hT_done")
            hT_ready = sem(n + "hT_ready")
            h_done = sem(n + "h_done")
            d_done = sem(n + "d_done")
            h_kept = sem(n + "h_kept")
            d_kept = sem(n + "d_kept")
            diag_ready = sem(n + "diag_ready")
            mean_done = sem(n + "mean_done")

            with nc.Block() as block:
                @block.sync
                def _(sp):
                    for i in range(4):
                        c = slice(i * T // 4, (i + 1) * T // 4)
                        sp.dma_start(x_all[:, c, :], x_view[:, c, :]).then_inc(x_loaded[i], 16)
                    sp.dma_start(W_sb[:], W_in).then_inc(w_loaded, 16)
                    sp.dma_start(a_two[:, 0:1], a_in[0:F, :]).then_inc(w_loaded, 16)
                    sp.dma_start(a_two[:, 1:2], a_in[F:2 * F, :]).then_inc(w_loaded, 16)
                    if first:
                        for q in range(Q):
                            sp.wait_ge(h_kept, q + 1)
                            sp.dma_start(h_view[:, q * QT:(q + 1) * QT, :], h_all[:, q * QT:(q + 1) * QT, 0:F])\
                                .then_inc(h_stored, 16)
                        sp.wait_ge(d_kept, Q)
                        sp.dma_start(d_mid, d_row[0:1, :]).then_inc(h_stored, 16)
                        sp.wait_ge(h_stored, 16 * (Q + 1))

                @block.vector
                def _(dve):
                    links = [0]

                    def link(ins):
                        links[0] += 1
                        ins.then_inc(chain, 1)
                        dve.wait_ge(chain, links[0])

                    for i in range(4):
                        dve.wait_ge(x_loaded[i], 16)
                        for t in range(i * T // 4, (i + 1) * T // 4):
                            last = nc.vector.bn_stats(st[:, t, :], x_all[:, t, :])
                    link(last)
                    link(nc.vector.tensor_tensor(mean, st[:, :, 1], st[:, :, 4], ALU.add))
                    link(nc.vector.tensor_scalar(mean, mean, 0.5, None, ALU.mult))
                    link(nc.vector.tensor_tensor(tmp, st[:, :, 1], st[:, :, 4], ALU.subtract))
                    link(nc.vector.tensor_tensor(tmp, tmp, tmp, ALU.mult))
                    link(nc.vector.tensor_tensor(var, st[:, :, 2], st[:, :, 5], ALU.add))
                    link(nc.vector.scalar_tensor_tensor(var, tmp, F / 4.0, var, ALU.mult, ALU.add))
                    nc.vector.tensor_scalar(var, var, 1.0 / F, EPS, ALU.mult, ALU.add).then_inc(var_ready, 1)
                    dve.wait_ge(std_ready, 1)
                    link(nc.vector.reciprocal(rstd, tmp2))
                    link(nc.vector.tensor_tensor(tmp, rstd, rstd, ALU.mult))
                    link(nc.vector.tensor_tensor(tmp, tmp, var, ALU.mult))
                    link(nc.vector.tensor_scalar(tmp, tmp, -0.5, 1.5, ALU.mult, ALU.add))
                    link(nc.vector.tensor_tensor(rstd, rstd, tmp, ALU.mult))
                    for t in range(T):
                        ins = nc.vector.tensor_scalar(hn[:, t, :], x_all[:, t, :], mean[:, t:t + 1], rstd[:, t:t + 1],
                                                      ALU.subtract, ALU.mult)
                        if t % QT == QT - 1:
                            ins.then_inc(hn_ready, 1)
                        if t == QT - 1:
                            dve.wait_ge(w_loaded, 48)
                            nc.vector.tensor_scalar(a_src_cols[:], ones[:], a_two[:, 0:1], None, ALU.mult)
                            nc.vector.tensor_scalar(a_dst_cols[:], ones[:], a_two[:, 1:2], None, ALU.mult)\
                                .then_inc(a_cols, 1)
                    for q in range(Q):
                        cols = slice(q * QN, (q + 1) * QN)
                        dve.wait_ge(h_done, q + 1)
                        nc.vector.tensor_copy(h_all[:, q * QT:(q + 1) * QT, 0:F],
                                              h_ps.rearrange("p (t f) -> p t f", f=F)).then_inc(h_kept, 1)
                        dve.wait_ge(d_done, q + 1)
                        nc.vector.tensor_reduce(d_max[:, q:q + 1], d_ps[:, 0:QN], AX.X, ALU.max)
                        nc.vector.tensor_reduce(d_min[:, q:q + 1], d_ps[:, 0:QN], AX.X, ALU.min)
                        if first:
                            link(nc.vector.tensor_scalar(inv, sum_ps[:, 0:QN], 0.0, None, ALU.is_equal, ALU.max,
                                                         accum_out=inv_any[:, q:q + 1]))
                            nc.vector.scalar_tensor_tensor(d_row[:, cols], inv, -NEVER, d_ps[:, 0:QN],
                                                           ALU.mult, ALU.add).then_inc(d_kept, 1)
                        else:
                            nc.vector.tensor_copy(d_row[:, cols], d_ps[:, 0:QN]).then_inc(d_kept, 1)
                    link(nc.vector.tensor_copy(sd_col[:], s_ps[:, 0:2 * T].rearrange("p (t k) -> p t k", k=2)))
                    link(nc.vector.tensor_reduce(top[:], d_max[:], AX.X, ALU.max))
                    link(nc.vector.tensor_reduce(low[:], d_min[:], AX.X, ALU.min))
                    link(nc.vector.tensor_scalar(base[:], low[:], -1.0, None, ALU.add))
                    link(nc.vector.tensor_scalar(exp_bias[:, 0:1], top[:], -1.0, SHIFT, ALU.mult, ALU.add))
                    link(nc.vector.tensor_scalar(exp_bias[:, 1:2], top[:], -ALPHA, SHIFT, ALU.mult, ALU.add))
                    link(nc.vector.tensor_scalar(exp_bias[:, 2:3], top[:], ALPHA - 1.0, None, ALU.mult))
                    link(nc.vector.tensor_scalar(lin[:], sd_col[:, :, 0], top[:, 0:1], 0.0, ALU.add, ALU.max))
                    link(nc.vector.tensor_tensor(flag[:, 0:1], top[:], low[:], ALU.subtract))
                    link(nc.vector.tensor_scalar(flag[:, 2:3], flag[:, 0:1], FAST_SPREAD, None, ALU.is_gt))
                    if first:
                        link(nc.vector.tensor_reduce(flag[:, 1:2], inv_any[:], AX.X, ALU.max))
                        link(nc.vector.tensor_tensor(flag[:, 2:3], flag[:, 2:3], flag[:, 1:2], ALU.max))
                    if first:
                        link(nc.vector.tensor_copy(edges_kept[:], flag[:, 2:3]))
                        link(nc.vector.tensor_copy(path_f[:, 0:1], flag[:, 2:3]))
                        link(nc.vector.tensor_copy(path[:, 0:1], path_f[:, 0:1]))
                    else:
                        link(nc.vector.tensor_tensor(path_f[:, 1:2], flag[:, 2:3], edges_kept[:], ALU.max))
                        link(nc.vector.tensor_copy(path[:, 1:2], path_f[:, 1:2]))
                    if not first:
                        dve.wait_ge(hT_ready, Q)
                        link(nc.vector.tensor_reduce(h_mean[:], h_sums[:], AX.X, ALU.add))
                        nc.vector.tensor_scalar(mean_diag, ident[:], h_mean[:, 0:1], 1.0 / N, ALU.mult, ALU.mult)\
                            .then_inc(diag_ready, 1)
                        dve.wait_ge(mean_done, 1)
                        nc.vector.tensor_copy(mean_row[:], hT_ps[:, 0:F])

                @block.scalar
                def _(act):
                    def keep_s(q):
                        act.wait_ge(d_done, q + 1)
                        nc.scalar.activation(s_row[:, q * QN:(q + 1) * QN], sr_ps, ACT.Identity).then_inc(s_kept, 1)

                    act.wait_ge(var_ready, 1)
                    nc.scalar.activation(tmp2, var, ACT.Sqrt).then_inc(std_ready, 1)
                    for q in range(Q):
                        act.wait_ge(hn_turned, q + 1)
                        if q >= 2:
                            act.wait_ge(h_done, q - 1)
                        nc.scalar.activation(hnT[q % 2], hn_ps[q % 2], ACT.Relu).then_inc(hnT_ready, 1)
                        act.wait_ge(hT_done, q + 1)
                        if q >= 2:
                            act.wait_ge(d_done, q - 1)
                        nc.scalar.activation(hT[q % 2], hT_ps[:, 0:QN], ACT.Identity,
                                             accum_out=h_sums[:, q:q + 1]).then_inc(hT_ready, 1)
                        if q >= 1:
                            keep_s(q - 1)
                    keep_s(Q - 1)

                @block.tensor
                def _(pe):
                    def turn_hn(q):
                        pe.wait_ge(hn_ready, q + 1)
                        if q >= 2:
                            pe.wait_ge(hnT_ready, q - 1)
                        for i in range(QT):
                            last = nc.tensor.transpose(hn_ps[q % 2][:, i * P:(i + 1) * P], hn[:, q * QT + i, :], ident[:])
                        last.then_inc(hn_turned, 1)

                    def products(q):
                        pe.wait_ge(hnT_ready, q + 1)
                        if q >= 1:
                            pe.wait_ge(hT_ready, q)
                        nc.tensor.matmul(hT_ps[:, 0:QN], W_sb[:], hnT[q % 2], start=True, stop=True).then_inc(hT_done, 1)
                        if q >= 1:
                            pe.wait_ge(h_kept, q)
                        for i in range(QT):
                            last = nc.tensor.matmul(h_ps[:, i * F:(i + 1) * F], hnT[q % 2][:, i * P:(i + 1) * P],
                                                    W_sb[:], start=True, stop=True)
                        last.then_inc(h_done, 1)

                    def scores(q):
                        pe.wait_ge(hT_ready, q + 1)
                        if q >= 1:
                            pe.wait_ge(d_kept, q)
                        if q == 0:
                            pe.wait_ge(a_cols, 1)
                        nc.tensor.matmul(d_ps[:, 0:QN], a_dst_cols[:], hT[q % 2], start=True, stop=True)
                        if q >= 1:
                            pe.wait_ge(s_kept, q)
                        nc.tensor.matmul(sr_ps[:, 0:QN], a_src_cols[:], hT[q % 2], start=True, stop=True)
                        if first:
                            nc.tensor.matmul(sum_ps[:, 0:QN], ones[:], hT[q % 2], start=True, stop=True)
                        for i in range(QT):
                            t = q * QT + i
                            last = nc.tensor.matmul(s_ps[:, 2 * t:2 * t + 2], hT[q % 2][:, i * P:(i + 1) * P], a_two[:],
                                                    start=True, stop=True)
                        last.then_inc(d_done, 1)

                    turn_hn(0)
                    pe.wait_ge(w_loaded, 48)
                    for q in range(Q):
                        if q + 1 < Q:
                            turn_hn(q + 1)
                        products(q)
                        if q >= 1:
                            scores(q - 1)
                    scores(Q - 1)
                    if not first:
                        pe.wait_ge(diag_ready, 1)
                        nc.tensor.matmul(hT_ps[:, 0:F], ones[:], mean_diag, start=True, stop=True)\
                            .then_inc(mean_done, 1)

        def general_path(layer, x_in, x_to):
            first = layer == 0
            n = f"g{layer}_"
            restored = sem(n + "restored")
            LK = 2 * NC
            adj_loaded = [sem(n + f"adj_loaded{i}") for i in range(ADJS)]
            row_link = sem(n + "row_link")
            adj_used = sem(n + "adj_used")
            probe_link = sem(n + "probe_link")
            probed = sem(n + "chunk_probed")
            m_ready = sem(n + "m_ready")
            lrelu_link = sem(n + "lrelu_link")
            lrelu_done = sem(n + "lrelu_done")
            e_ready = sem(n + "e_ready")
            thresholded = sem(n + "thresholded")
            turned = sem(n + "unit_turned")
            by_act = sem(n + "wT_by_act")
            summed = sem(n + "unit_summed")
            acc_read = sem(n + "acc_read")
            y_neg_ready = sem(n + "y_neg_ready")
            y_exp_ready = sem(n + "y_exp_ready")
            rest_link = sem(n + "rest_link")
            res_loaded = [sem(n + f"res_loaded{i}") for i in range(ACCS)]
            out_ready = sem(n + "out_ready")
            stored = [sem(n + f"stored{i}") for i in range(ACCS)]
            tile_link = sem(n + "tile_link")
            finish_link = sem(n + "finish_link")
            SHIFT_LINKS = 4
            TILE_LINKS = SHIFT_LINKS + (3 if first else 1)
            FINISH_LINKS = 3
            RES = 32 if first else 16

            x_view = x_in.rearrange("(t p) f -> t p f", p=P)
            h_view = h_mid.rearrange("(t p) f -> t p f", p=P)
            out_view = x_to.rearrange("(t p) f -> t p f", p=P)
            adj_view = adj.rearrange("(t p) (c n) -> t p c n", p=P, n=CH)

            def chunk(c):
                return slice(c * CH, (c + 1) * CH)

            def steps(eng, step):
                for st in range(LEAD):
                    step(0, st)
                with eng.Fori(0, LOOPS) as it:
                    for r in range(UN):
                        step(it, LEAD + r)
                for st in range(LEAD + LOOPS * UN, T + 3):
                    step(0, st)

            def wait(eng, sm, it, per_step, value):
                if value > 0:
                    eng.wait_ge(sm, it * (UN * per_step) + value)

            def runs(st, lag):
                return 0 <= st - lag < T

            def wait_adj(eng, it, st, i):
                no = st * LK + i
                eng.wait_ge(adj_loaded[no % ADJS], it * (UN * LK // ADJS * 16) + (no // ADJS + 1) * 16)

            def wait_slot(eng, it, st, c):
                wait(eng, turned, it, U, (st - SLOTS) * U + (c + 1) * UC if st >= SLOTS else 0)

            def wait_moved(eng, it, st, u):
                if u < 0:
                    st, u = st - 1, u + U
                wait(eng, by_act, it, U, (st - 1) * U + u + 1 if st >= 1 else 0)

            def sync_rows(sp):
                def step(it, st):
                    for i in range(LK):
                        if runs(st, 0):
                            no = st * LK + i
                            wait(sp, adj_used, it, LK, no - ADJS + 1)
                            sp.dma_start(adj_buf[no % ADJS], adj_view[it * UN + st, :, i % NC, :])\
                                .then_inc(adj_loaded[no % ADJS], 16)
                        if i == 2 and runs(st, 3):
                            b = (st - 3) % ACCS
                            wait(sp, out_ready, it, 1, st - 2)
                            sp.dma_start(out_view[it * UN + (st - 3)], x_out[:, b]).then_inc(stored[b], 16)
                        if i == 3 and runs(st, 1):
                            b = (st - 1) % ACCS
                            wait(sp, out_ready, it, 1, st - ACCS)
                            sp.dma_start(x_res[:, b], x_view[it * UN + (st - 1)]).then_inc(res_loaded[b], 16)
                            if first:
                                sp.dma_start(h_res[:, b], h_view[it * UN + (st - 1)]).then_inc(res_loaded[b], 16)

                if first:
                    sp.dma_start(h_all[:, :, 0:F], h_mid.rearrange("(t p) f -> p t f", p=P)).then_inc(restored, 16)
                    sp.dma_start(d_row, d_mid.partition_broadcast(P)).then_inc(restored, 16)
                steps(sp, step)
                for b in range(ACCS):
                    sp.wait_ge(stored[b], 16 * len(range(b, T, ACCS)))

            def scalar_rows(act):
                def move_unit(it, st, u):
                    if runs(st, 1):
                        wait(act, turned, it, U, (st - 1) * U + u + 1)
                        wait(act, summed, it, U, (st - 1) * U + u - 1)
                        nc.scalar.activation(wT[u % 2], turn[u % 2], ACT.Identity)\
                            .then_inc(by_act, 1)

                def step(it, st):
                    for c in range(NC):
                        for u in range(c * UC, (c + 1) * UC):
                            move_unit(it, st, u)
                        if first and c == 1 and runs(st, 2):
                            wait(act, acc_read, it, 1, st - 1)
                            wait(act, rest_link, it, 2, (st - 3) * 2 + 1)
                            nc.scalar.activation(y_exp[:], y[:], ACT.Relu, scale=-1.0).then_inc(y_neg_ready, 1)
                            wait(act, y_neg_ready, it, 1, st - 1)
                            nc.scalar.activation(y_exp[:], y_exp[:], ACT.Exp, scale=-1.0).then_inc(y_exp_ready, 1)
                    if runs(st, 0):
                        wait(act, m_ready, it, 1, st + 1)
                        for c in range(NC):
                            w = weights[st % SLOTS][:, chunk(c)]
                            wait(act, lrelu_done, it, NC, st * NC + c + 1)
                            nc.scalar.activation(w, w, ACT.Exp, bias=neg_m[:, st % SLOTS:st % SLOTS + 1])\
                                .then_inc(e_ready, 1)

                steps(act, step)

            def tensor_rows(pe):
                def turn_unit(it, st, u):
                    if u % UC == 0:
                        c = u // UC
                        if first:
                            wait(pe, thresholded, it, NC, (st - 1) * NC + c + 1)
                        else:
                            wait(pe, adj_used, it, LK, (st - 1) * LK + LK - NC + c + 1)
                    wait_moved(pe, it, st, u - 2)
                    for b in range(UJ):
                        j = (u * UJ + b) * P
                        last = nc.tensor.transpose(turn[u % 2][:, b * P:(b + 1) * P],
                                                   weights[(st - 1) % SLOTS][:, j:j + P], ident[:])
                    last.then_inc(turned, 1)

                def sum_unit(it, st, u):
                    wait_moved(pe, it, st, u)
                    if u == 0:
                        wait(pe, acc_read, it, 1, st - ACCS)
                    for b in range(UJ):
                        j = u * UJ + b
                        last = nc.tensor.matmul(acc[(st - 1) % ACCS][:, 0:F], wT[u % 2][:, b * P:(b + 1) * P],
                                                h_all[:, j, 0:F], start=(j == 0), stop=(j == T - 1))
                    last.then_inc(summed, 1)

                def step(it, st):
                    if runs(st, 1):
                        for u in range(U + 1):
                            if u < U:
                                turn_unit(it, st, u)
                            if u >= 1:
                                sum_unit(it, st, u - 1)

                if first:
                    pe.wait_ge(restored, 32)
                steps(pe, step)

            def vector_rows(dve):
                def link(ins, sm, it, per_step, value):
                    ins.then_inc(sm, 1)
                    wait(dve, sm, it, per_step, value)

                def tlink(ins, it, st, i):
                    link(ins, tile_link, it, TILE_LINKS, st * TILE_LINKS + i)

                def flink(ins, it, st, i):
                    link(ins, finish_link, it, FINISH_LINKS, (st - 2) * FINISH_LINKS + i)

                def probe(it, st, c):
                    w = weights[st % SLOTS][:, chunk(c)]
                    wait_adj(dve, it, st, c)
                    wait_slot(dve, it, st, c)
                    nc.vector.scalar_tensor_tensor(w, adj_buf[(st * LK + c) % ADJS], 0.0, row2[:, chunk(c)],
                                                   ALU.is_gt, ALU.mult).then_inc(adj_used, 1)
                    wait(dve, adj_used, it, LK, st * LK + c + 1)
                    nc.vector.tensor_reduce(v_part[:, c:c + 1], w, AX.X, ALU.max).then_inc(probe_link, 1)
                    wait(dve, probe_link, it, NC, st * NC + c + 1)
                    nc.vector.tensor_scalar(w, w, 0.0, None, ALU.is_gt, ALU.add,
                                            accum_out=cnt_part[:, st % SLOTS, c:c + 1]).then_inc(probed, 1)

                def shift(it, st):
                    wait(dve, probed, it, NC, (st + 1) * NC)
                    tlink(nc.vector.tensor_reduce(v_top[:, 0:1], v_part[:], AX.X, ALU.max), it, st, 1)
                    tlink(nc.vector.tensor_scalar(v_top[:, 1:2], v_top[:, 0:1], base[:, 0:1], None, ALU.add),
                          it, st, 2)
                    tlink(nc.vector.tensor_tensor(v_top[:, 2:3], v_top[:, 1:2],
                                                  sd_col[:, bass.ds(it * UN + st, 1), 0], ALU.add), it, st, 3)
                    tlink(nc.vector.scalar_tensor_tensor(v_top[:, 3:4], v_top[:, 2:3], ALPHA, v_top[:, 2:3],
                                                         ALU.mult, ALU.max), it, st, 4)
                    nc.vector.tensor_scalar(neg_m[:, st % SLOTS:st % SLOTS + 1], v_top[:, 3:4], -1.0, -MARGIN,
                                            ALU.mult, ALU.add).then_inc(m_ready, 1)

                def lrelu(it, st, c):
                    w = weights[st % SLOTS][:, chunk(c)]
                    nc.vector.tensor_scalar(w, d_row[:, chunk(c)], sd_col[:, bass.ds(it * UN + st, 1), 0], None,
                                            ALU.add).then_inc(lrelu_link, 1)
                    wait(dve, lrelu_link, it, NC, st * NC + c + 1)
                    nc.vector.scalar_tensor_tensor(w, w, ALPHA, w, ALU.mult, ALU.max).then_inc(lrelu_done, 1)

                def mask(it, st, c):
                    w = weights[st % SLOTS][:, chunk(c)]
                    wait_adj(dve, it, st, NC + c)
                    wait(dve, e_ready, it, NC, st * NC + c + 1)
                    nc.vector.scalar_tensor_tensor(w, adj_buf[(st * LK + NC + c) % ADJS], 0.0, w, ALU.max, ALU.min,
                                                   accum_out=z_part[:, st % SLOTS, c:c + 1]).then_inc(adj_used, 1)

                def row_sums(it, st):
                    b = slice(st % UN, st % UN + 1)
                    wait(dve, adj_used, it, LK, (st + 1) * LK)
                    if first:
                        tlink(nc.vector.tensor_reduce(n_edges[:, b], cnt_part[:, st % SLOTS, :], AX.X, ALU.add),
                              it, st, SHIFT_LINKS + 1)
                    ins = nc.vector.tensor_reduce(z_sum[:, b], z_part[:, st % SLOTS, :], AX.X, ALU.add)
                    if first:
                        tlink(ins, it, st, SHIFT_LINKS + 2)
                        tlink(nc.vector.tensor_scalar(theta[:, b], z_sum[:, b], THR, None, ALU.mult),
                              it, st, SHIFT_LINKS + 3)
                    else:
                        tlink(ins, it, st, SHIFT_LINKS + 1)

                def threshold(it, st, c):
                    w = weights[st % SLOTS][:, chunk(c)]
                    nc.vector.scalar_tensor_tensor(w, w, theta[:, st % UN:st % UN + 1], w, ALU.is_ge, ALU.mult)\
                        .then_inc(thresholded, 1)

                def finish(it, st):
                    g = st - 2
                    a = acc[g % ACCS]
                    b = slice(g % UN, g % UN + 1)
                    z = z_sum[:, b]
                    wait(dve, summed, it, U, (g + 1) * U)
                    flink(nc.vector.tensor_scalar(scale[:, b], z, SMALL, None, ALU.max), it, st, 1)
                    flink(nc.vector.reciprocal(scale[:, b], scale[:, b]), it, st, 2)
                    no = g // ACCS
                    dve.wait_ge(res_loaded[g % ACCS], it * (UN // ACCS * RES) + (no + 1) * RES)
                    if first:
                        flink(nc.vector.tensor_tensor(scale[:, b], scale[:, b], n_edges[:, b], ALU.mult), it, st, 3)
                        wait(dve, y_exp_ready, it, 1, g)
                        nc.vector.scalar_tensor_tensor(y[:], a[:, 0:F], scale[:, b], h_res[:, g % ACCS],
                                                       ALU.mult, ALU.add).then_inc(acc_read, 1)
                        return
                    if no >= 1:
                        dve.wait_ge(stored[g % ACCS], it * (UN // ACCS * 16) + no * 16)
                    flink(nc.vector.tensor_scalar(empty[:, b], z, 0.0, None, ALU.is_le), it, st, 3)
                    nc.vector.scalar_tensor_tensor(x_out[:, g % ACCS], a[:, 0:F], scale[:, b], x_res[:, g % ACCS],
                                                   ALU.mult, ALU.add).then_inc(acc_read, 1)
                    wait(dve, acc_read, it, 1, g + 1)
                    nc.vector.scalar_tensor_tensor(x_out[:, g % ACCS], mean_row[:], empty[:, b], x_out[:, g % ACCS],
                                                   ALU.mult, ALU.add).then_inc(out_ready, 1)

                def finish_elu(it, st):
                    g = st - 2
                    wait(dve, y_exp_ready, it, 1, g + 1)
                    link(nc.vector.tensor_scalar(rest[:], y_exp[:], -1.0, None, ALU.add),
                         rest_link, it, 2, g * 2 + 1)
                    if g >= ACCS:
                        dve.wait_ge(stored[g % ACCS], it * (UN // ACCS * 16) + g // ACCS * 16)
                    link(nc.vector.scalar_tensor_tensor(rest[:], y[:], 0.0, rest[:], ALU.max, ALU.add),
                         rest_link, it, 2, g * 2 + 2)
                    nc.vector.tensor_tensor(x_out[:, g % ACCS], rest[:], x_res[:, g % ACCS], ALU.add)\
                        .then_inc(out_ready, 1)

                def step(it, st):
                    makes, finishes = runs(st, 0), runs(st, 2)
                    if finishes:
                        finish(it, st)
                    if makes:
                        for c in range(NC):
                            probe(it, st, c)
                        shift(it, st)
                        for c in range(NC):
                            lrelu(it, st, c)
                        for c in range(NC):
                            mask(it, st, c)
                        row_sums(it, st)
                        if first:
                            for c in range(NC):
                                threshold(it, st, c)
                    if first and finishes:
                        finish_elu(it, st)

                if first:
                    dve.wait_ge(restored, 32)
                nc.vector.tensor_scalar(row2, d_row, base[:, 0:1], 0.0, ALU.subtract, ALU.max).then_inc(row_link, 1)
                dve.wait_ge(row_link, 1)
                steps(dve, step)

            return sync_rows, scalar_rows, tensor_rows, vector_rows


        def wait_in(eng, sm, it, per_group, value):
            if value > 0:
                eng.wait_ge(sm, it * (2 * per_group) + value)

        def groups_of(eng, groups, group):
            group(0, 0)
            group(0, 1)
            with eng.Fori(0, (groups - 4) // 2) as it:
                group(it, 2)
                group(it, 3)
            group(0, groups - 2)
            group(0, groups - 1)

        def acc_tile(group, tiles, k):
            first_bank = (4 if tiles == G0 else 0) + group % 2 * (tiles // 2)
            b = bank(first_bank + k // 2)
            return b[:, k % 2 * 256:k % 2 * 256 + FZ]

        def fold_scalar(act, folded, r_ready):
            nc.scalar.activation(r_col[:], lin[:], ACT.Exp, scale=ALPHA - 1.0)
            nc.scalar.activation(rho_col[:], sd_col[:, :, 1], ACT.Exp, scale=1.0 - ALPHA, bias=exp_bias[:, 2:3])
            nc.scalar.activation(low_exp[:, 0:1], low[:], ACT.Exp, scale=ALPHA, bias=exp_bias[:, 1:2])
            nc.scalar.activation(low_exp[:, 1:2], low[:], ACT.Exp, scale=1.0 - ALPHA, bias=exp_bias[:, 2:3])
            nc.scalar.activation(D_col[:], sd_col[:, :, 1], ACT.Exp, scale=ALPHA, bias=exp_bias[:, 1:2])\
                .then_inc(folded, 1)
            for c in range(NC):
                act.wait_ge(folded, c + 2)
                cols = s_row[:, c * CH:(c + 1) * CH]
                ins = nc.scalar.activation(cols, cols, ACT.Exp, scale=ALPHA - 1.0)
            ins.then_inc(r_ready, 1)

        def fold_vector(dve, folded, h_folded):
            dve.wait_ge(folded, 1)
            for c in range(NC):
                cols = s_row[:, c * CH:(c + 1) * CH]
                nc.vector.tensor_scalar(cols, cols, top[:, 0:1], 0.0, ALU.add, ALU.max).then_inc(folded, 1)
            D = D_col[:].rearrange("p (t o) -> p t o", o=1)
            nc.vector.tensor_tensor(h_all[:, :, 0:F], h_all[:, :, 0:F], D.to_broadcast([P, T, F]), ALU.mult)
            nc.vector.tensor_copy(h_all[:, :, F:FZ], D).then_inc(h_folded, 1)

        def fast_path_0(x_in, x_to):
            n = "f0_"
            folded = sem(n + "folded")
            h_folded = sem(n + "h_folded")
            r_ready = sem(n + "r_ready")
            adj_loaded = [sem(n + f"adj_loaded{i}") for i in range(G0)]
            masked = sem(n + "masked")
            counted = sem(n + "counted")
            turned = sem(n + "turned")
            formed = sem(n + "formed")
            copied = sem(n + "copied")
            summed = sem(n + "summed")
            edges_stored = [sem(n + f"edges_stored{i}") for i in range(2)]
            counts_read = sem(n + "counts_read")
            acc_read = sem(n + "acc_read")
            y_neg_ready = sem(n + "y_neg_ready")
            y_exp_ready = sem(n + "y_exp_ready")
            res_loaded = sem(n + "res_loaded")
            out_ready = sem(n + "out_ready")
            stored = sem(n + "stored")
            chain = sem(n + "finish_chain")
            LINKS = 7

            assert G0 * CH <= N
            adj_in = [part(i * CH, CH).bitcast(I32) for i in range(G0)]
            at = 2 * N
            edges = [part(at + i * GI * CB // 2, GI * CB // 2).bitcast(BF16).rearrange("p (t c) -> p t c", t=G0)
                     for i in range(2)]
            at += GI * CB
            wTs = [part(at + i * 2 * GI, 2 * GI) for i in range(RING)]
            at += RING * 2 * GI
            edge_out = [part(at + i * CB * GI // 4, CB * GI // 4).bitcast(U8) for i in range(2)]
            at += CB * GI // 2
            copies = part(at, CH // 2).bitcast(BF16)
            at += CH // 2
            cnt = [part(at + i * G0 * NC, G0 * NC).rearrange("p (t c) -> p t c", c=NC) for i in range(2)]
            at += 2 * G0 * NC
            ne, zs, fl = [part(at + i * G0, G0) for i in range(3)]
            at += 3 * G0
            xr, hr, yy, ye, xo = [part(at + i * GI, GI) for i in range(5)]
            at += 5 * GI
            assert at <= 5 * N
            edge_ps = [bank(i).bitcast(BF16) for i in range(RING)]

            x_view = x_in.rearrange("(g t p) f -> g p t f", p=P, t=G0)
            h_view = h_mid.rearrange("(g t p) f -> g p t f", p=P, t=G0)
            out_view = x_to.rearrange("(g t p) f -> g p t f", p=P, t=G0)
            adj_view = adj.rearrange("(t p) (c n) -> t p c n", p=P, n=CH)

            def sync_rows(sp):
                def group(it, g):
                    for c in range(NC):
                        for k in range(G0):
                            u = g * NC + c
                            wait_in(sp, masked, it, NC * G0, (u - 1) * G0 + k + 1)
                            sp.dma_start(adj_in[k], adj_view[it * (2 * G0) + (g * G0 + k), :, c, :])\
                                .then_inc(adj_loaded[k], 16)
                        if g * NC + c >= 2:
                            store_edges(it, g, c - 2)
                        if c == 2:
                            if g >= 1:
                                wait_in(sp, out_ready, it, 1, g)
                                sp.dma_start(out_view[it * 2 + (g - 1)], xo.rearrange("p (t f) -> p t f", t=G0))\
                                    .then_inc(stored, 16)
                            sp.dma_start(xr.rearrange("p (t f) -> p t f", t=G0), x_view[it * 2 + g])\
                                .then_inc(res_loaded, 16)
                            sp.dma_start(hr.rearrange("p (t f) -> p t f", t=G0), h_view[it * 2 + g])\
                                .then_inc(res_loaded, 16)

                def store_edges(it, g, c):
                    if c < 0:
                        g, c = g - 1, c + NC
                    wait_in(sp, copied, it, PAIRS, g * PAIRS + (c + 1) * CP)
                    sp.dma_start(edgesT[it * (2 * NC) + (g * NC + c)], edge_out[c % 2]).then_inc(edges_stored[c % 2], 16)

                groups_of(sp, NG, group)
                store_edges(0, NG - 1, NC - 2)
                store_edges(0, NG - 1, NC - 1)
                sp.wait_ge(out_ready, NG)
                sp.dma_start(out_view[NG - 1], xo.rearrange("p (t f) -> p t f", t=G0)).then_inc(stored, 16)
                sp.wait_ge(stored, 16 * NG)
                for i in range(2):
                    sp.wait_ge(edges_stored[i], 16 * NG * NC // 2)

            def scalar_rows(act):
                def count(it, g, c, k):
                    if c >= NC:
                        g, c = g + 1, c - NC
                    if g >= NG:
                        return
                    u = g * NC + c
                    wait_in(act, masked, it, NC * G0, u * G0 + k + 1)
                    wait_in(act, counted, it, NC * G0, u * G0 + k)
                    if c == 0 and k == 0:
                        wait_in(act, counts_read, it, 1, g - 1)
                    nc.scalar.activation(copies, edges[c % 2][:, k, :], ACT.Identity,
                                         accum_out=cnt[g % 2][:, k, c:c + 1]).then_inc(counted, 1)

                def group(it, g):
                    for p in range(PAIRS):
                        c, q = p // CP, p % CP
                        m = g * PAIRS + p
                        wait_in(act, formed, it, 2 * PAIRS, 2 * (m + 1))
                        if q == 0 and g * NC + c >= 2:
                            act.wait_ge(edges_stored[c % 2], it * (NC * 16) + (g * NC + c) // 2 * 16)
                        nc.scalar.activation(edge_out[c % 2][:, q * 2 * GI:(q + 1) * 2 * GI], edge_ps[m % RING],
                                             ACT.Identity).then_inc(copied, 1)
                        if q < G0:
                            count(it, g, c + 1, q)
                        if p == 9 and g >= 1:
                            elu(it, g - 1)

                def elu(it, g):
                    wait_in(act, acc_read, it, 1, g + 1)
                    nc.scalar.activation(ye, yy, ACT.Relu, scale=-1.0).then_inc(y_neg_ready, 1)
                    wait_in(act, y_neg_ready, it, 1, g + 1)
                    nc.scalar.activation(ye, ye, ACT.Exp, scale=-1.0).then_inc(y_exp_ready, 1)

                fold_scalar(act, folded, r_ready)
                for k in range(G0):
                    count(0, 0, 0, k)
                groups_of(act, NG, group)
                elu(0, NG - 1)

            def tensor_rows(pe):
                def turn_pair(it, g, p):
                    if p >= PAIRS:
                        g, p = g + 1, p - PAIRS
                    if g >= NG:
                        return
                    c, q = p // CP, p % CP
                    m = g * PAIRS + p
                    if q == 0:
                        wait_in(pe, masked, it, NC * G0, (g * NC + c + 1) * G0)
                    wait_in(pe, copied, it, PAIRS, m - RING + 1)
                    for b in range(2):
                        for k in range(G0):
                            last = nc.tensor.transpose(edge_ps[m % RING][:, (b * G0 + k) * P:(b * G0 + k + 1) * P],
                                                       edges[c % 2][:, k, (2 * q + b) * P:(2 * q + b + 1) * P],
                                                       identb[:])
                    last.then_inc(turned, 1)

                def sum_pair(it, g, p):
                    m = g * PAIRS + p
                    if p == 0:
                        wait_in(pe, acc_read, it, 1, g - 1)
                    for b in range(2):
                        j = 2 * p + b
                        wait_in(pe, formed, it, 2 * PAIRS, m * 2 + b + 1)
                        for k in range(G0):
                            last = nc.tensor.matmul(acc_tile(g, G0, k), wTs[m % RING][:, b * GI + k * P:b * GI + (k + 1) * P],
                                                    h_all[:, j, :], start=(j == 0 and k % 2 == 0), stop=(j == T - 1),
                                                    skip_group_check=True)
                    last.then_inc(summed, 1)

                def group(it, g):
                    for p in range(PAIRS):
                        turn_pair(it, g, p + 2)
                        sum_pair(it, g, p)

                turn_pair(0, 0, 0)
                turn_pair(0, 0, 1)
                pe.wait_ge(h_folded, 1)
                groups_of(pe, NG, group)

            def vector_rows(dve):
                def mark(it, g, c, k):
                    if c >= NC:
                        g, c = g + 1, c - NC
                    if g >= NG:
                        return
                    u = g * NC + c
                    dve.wait_ge(adj_loaded[k], it * (2 * NC * 16) + (u + 1) * 16)
                    wait_in(dve, turned, it, PAIRS, (u - 1) * CP)
                    wait_in(dve, counted, it, NC * G0, (u - 2) * G0 + k + 1)
                    nc.vector.tensor_scalar(edges[c % 2][:, k, :], adj_in[k], 0.0, None, ALU.is_gt).then_inc(masked, 1)

                def form(it, g, p):
                    m = g * PAIRS + p
                    wait_in(dve, turned, it, PAIRS, m + 1)
                    wait_in(dve, summed, it, PAIRS, m - RING + 1)
                    for b in range(2):
                        nc.vector.scalar_tensor_tensor(wTs[m % RING][:, b * GI:(b + 1) * GI],
                                                       s_row[:, bass.ds(it * (2 * GI) + g * GI, GI)],
                                                       rho_col[:, 2 * p + b:2 * p + b + 1],
                                                       edge_ps[m % RING][:, b * GI:(b + 1) * GI],
                                                       ALU.max, ALU.mult).then_inc(formed, 1)

                def link(ins, it, g, i):
                    ins.then_inc(chain, 1)
                    wait_in(dve, chain, it, LINKS, g * LINKS + i)

                def finish(it, g):
                    four = bass.ds(it * (2 * G0) + g * G0, G0)
                    wait_in(dve, summed, it, PAIRS, (g + 1) * PAIRS)
                    wait_in(dve, counted, it, NC * G0, (g + 1) * NC * G0)
                    nc.vector.tensor_reduce(ne, cnt[g % 2], AX.X, ALU.add).then_inc(counts_read, 1)
                    for k in range(G0):
                        last = nc.vector.tensor_copy(zs[:, k:k + 1], acc_tile(g, G0, k)[:, F:FZ])
                    link(last, it, g, 1)
                    link(nc.vector.tensor_scalar(fl, r_col[:, four], low_exp[:, 1:2], low_exp[:, 0:1],
                                                 ALU.max, ALU.mult), it, g, 2)
                    nc.vector.scalar_tensor_tensor(at_risk[:, four], zs, THR * 1.001, fl, ALU.mult, ALU.is_gt)
                    link(nc.vector.tensor_scalar(zs, zs, SMALL, None, ALU.max), it, g, 3)
                    link(nc.vector.reciprocal(zs, zs), it, g, 4)
                    wait_in(dve, counts_read, it, 1, g + 1)
                    link(nc.vector.tensor_tensor(zs, zs, ne, ALU.mult), it, g, 5)
                    dve.wait_ge(res_loaded, it * 64 + (g + 1) * 32)
                    for k in range(G0):
                        cols = slice(k * F, (k + 1) * F)
                        last = nc.vector.scalar_tensor_tensor(yy[:, cols], acc_tile(g, G0, k)[:, 0:F], zs[:, k:k + 1],
                                                              hr[:, cols], ALU.mult, ALU.add)
                    last.then_inc(acc_read, 1)

                def finish_elu(it, g):
                    wait_in(dve, y_exp_ready, it, 1, g + 1)
                    link(nc.vector.tensor_scalar(ye, ye, -1.0, None, ALU.add), it, g, 6)
                    link(nc.vector.scalar_tensor_tensor(ye, yy, 0.0, ye, ALU.max, ALU.add), it, g, 7)
                    if g >= 1:
                        dve.wait_ge(stored, it * 32 + g * 16)
                    nc.vector.tensor_tensor(xo, ye, xr, ALU.add).then_inc(out_ready, 1)

                def group(it, g):
                    for p in range(PAIRS):
                        c, q = p // CP, p % CP
                        form(it, g, p)
                        if q < G0:
                            mark(it, g, c + 1, q)
                        if p == 5 and g >= 1:
                            finish(it, g - 1)
                        if p == 11 and g >= 1:
                            finish_elu(it, g - 1)

                fold_vector(dve, folded, h_folded)
                for k in range(G0):
                    mark(0, 0, 0, k)
                dve.wait_ge(r_ready, 1)
                groups_of(dve, NG, group)
                finish(0, NG - 1)
                finish_elu(0, NG - 1)
                dve.wait_ge(out_ready, NG)
                nc.vector.tensor_reduce(flag[:, 0:1], at_risk[:], AX.X, ALU.max)

            return sync_rows, scalar_rows, tensor_rows, vector_rows

        def weigh_risk():
            ready, counted = sem("risk_counted"), sem("risk_flagged")
            with nc.Block() as block:
                @block.tensor
                def _(pe):
                    nc.tensor.matmul(spare[:, 0:1], ones[:], flag[:, 0:1], start=True, stop=True).then_inc(ready, 1)

                @block.vector
                def _(dve):
                    dve.wait_ge(ready, 1)
                    nc.vector.tensor_scalar(flag[:, 1:2], spare[:, 0:1], 0.0, None, ALU.is_gt).then_inc(counted, 1)
                    dve.wait_ge(counted, 1)
                    nc.vector.tensor_tensor(path_f[:, 0:1], edges_kept[:], flag[:, 1:2], ALU.max).then_inc(counted, 1)
                    dve.wait_ge(counted, 2)
                    nc.vector.tensor_copy(path[:, 0:1], path_f[:, 0:1])

        def fast_path_1(x_in, x_to):
            n = "f1_"
            NG1 = T // G1
            R1 = G1 * P
            folded = sem(n + "folded")
            h_folded = sem(n + "h_folded")
            r_ready = sem(n + "r_ready")
            edges_loaded = [sem(n + f"edges_loaded{i}") for i in range(2)]
            formed = sem(n + "formed")
            summed = sem(n + "summed")
            acc_read = sem(n + "acc_read")
            res_loaded = sem(n + "res_loaded")
            out_ready = sem(n + "out_ready")
            stored = sem(n + "stored")
            chain = sem(n + "finish_chain")
            LINKS = 5

            at = 2 * N
            edges = [part(at + i * CB * R1 // 4, CB * R1 // 4).bitcast(U8)
                     .rearrange("p (h b i) -> p h b i", h=2, b=CB) for i in range(2)]
            at += CB * R1 // 2
            wTs = [part(at + i * R1, R1) for i in range(RING)]
            at += RING * R1
            zs, em = [part(at + i * G1, G1) for i in range(2)]
            at += 2 * G1
            xr, xo = [part(at + i * G1 * F, G1 * F) for i in range(2)]
            at += 2 * G1 * F
            assert at <= 5 * N

            x_view = x_in.rearrange("(g t p) f -> g p t f", p=P, t=G1)
            out_view = x_to.rearrange("(g t p) f -> g p t f", p=P, t=G1)

            def sync_rows(sp):
                def group(it, g):
                    for c in range(NC):
                        u = g * NC + c
                        wait_in(sp, formed, it, T, (u - 1) * CB)
                        for h in range(2):
                            sp.dma_start(edges[c % 2][:, h].rearrange("p b i -> p (b i)"),
                                         edgesT[it * (4 * NC) + ((2 * g + h) * NC + c)]).then_inc(edges_loaded[c % 2], 16)
                        if c == 2:
                            if g >= 1:
                                wait_in(sp, out_ready, it, 1, g)
                                sp.dma_start(out_view[it * 2 + (g - 1)], xo.rearrange("p (t f) -> p t f", t=G1))\
                                    .then_inc(stored, 16)
                            sp.dma_start(xr.rearrange("p (t f) -> p t f", t=G1), x_view[it * 2 + g])\
                                .then_inc(res_loaded, 16)

                groups_of(sp, NG1, group)
                sp.wait_ge(out_ready, NG1)
                sp.dma_start(out_view[NG1 - 1], xo.rearrange("p (t f) -> p t f", t=G1)).then_inc(stored, 16)
                sp.wait_ge(stored, 16 * NG1)

            def scalar_rows(act):
                fold_scalar(act, folded, r_ready)

            def tensor_rows(pe):
                def group(it, g):
                    for j in range(T):
                        m = g * T + j
                        if j == 0:
                            wait_in(pe, acc_read, it, 1, g - 1)
                        wait_in(pe, formed, it, T, m + 1)
                        for k in range(G1):
                            last = nc.tensor.matmul(acc_tile(g, G1, k), wTs[m % RING][:, k * P:(k + 1) * P],
                                                    h_all[:, j, :], start=(j == 0 and k % 2 == 0), stop=(j == T - 1),
                                                    skip_group_check=True)
                        last.then_inc(summed, 1)

                pe.wait_ge(h_folded, 1)
                groups_of(pe, NG1, group)

            def vector_rows(dve):
                def form(it, g, j):
                    m = g * T + j
                    c, b = j // CB, j % CB
                    if b == 0:
                        u = g * NC + c
                        dve.wait_ge(edges_loaded[c % 2], it * (NC * 32) + (u // 2 + 1) * 32)
                    wait_in(dve, summed, it, T, m - RING + 1)
                    nc.vector.scalar_tensor_tensor(wTs[m % RING].rearrange("p (h i) -> p h i", h=2),
                                                   s_row[:, bass.ds(it * (2 * R1) + g * R1, R1)]
                                                   .rearrange("p (h i) -> p h i", h=2),
                                                   rho_col[:, j:j + 1], edges[c % 2][:, :, b, :],
                                                   ALU.max, ALU.mult).then_inc(formed, 1)

                def link(ins, it, g, i):
                    ins.then_inc(chain, 1)
                    wait_in(dve, chain, it, LINKS, g * LINKS + i)

                def finish(it, g):
                    wait_in(dve, summed, it, T, (g + 1) * T)
                    for k in range(G1):
                        last = nc.vector.tensor_copy(zs[:, k:k + 1], acc_tile(g, G1, k)[:, F:FZ])
                    link(last, it, g, 1)
                    link(nc.vector.tensor_scalar(em, zs, 0.0, None, ALU.is_le), it, g, 2)
                    link(nc.vector.tensor_scalar(zs, zs, SMALL, None, ALU.max), it, g, 3)
                    link(nc.vector.reciprocal(zs, zs), it, g, 4)
                    dve.wait_ge(res_loaded, it * 32 + (g + 1) * 16)
                    for k in range(G1):
                        cols = slice(k * F, (k + 1) * F)
                        last = nc.vector.scalar_tensor_tensor(xr[:, cols], mean_row[:], em[:, k:k + 1], xr[:, cols],
                                                              ALU.mult, ALU.add)
                    link(last, it, g, 5)
                    if g >= 1:
                        dve.wait_ge(stored, it * 32 + g * 16)
                    for k in range(G1):
                        cols = slice(k * F, (k + 1) * F)
                        last = nc.vector.scalar_tensor_tensor(xo[:, cols], acc_tile(g, G1, k)[:, 0:F], zs[:, k:k + 1],
                                                              xr[:, cols], ALU.mult, ALU.add)
                    last.then_inc(acc_read, 1)
                    wait_in(dve, acc_read, it, 1, g + 1)
                    nc.vector.tensor_copy(em[:, 0:1], zs[:, 0:1]).then_inc(out_ready, 1)

                def group(it, g):
                    for j in range(T):
                        form(it, g, j)
                        if j == 3 and g >= 1:
                            finish(it, g - 1)

                fold_vector(dve, folded, h_folded)
                dve.wait_ge(r_ready, 1)
                groups_of(dve, NG1, group)
                finish(0, NG1 - 1)

            return sync_rows, scalar_rows, tensor_rows, vector_rows

        def run_paths(layer, fast, general):
            def unless_flagged(eng, which):
                flagged = eng.value_load(path[0:1, layer:layer + 1], min_val=0, max_val=1)
                with eng.If(flagged < 1):
                    fast[which](eng)

            def if_flagged(eng, which):
                flagged = eng.value_load(path[0:1, layer:layer + 1], min_val=0, max_val=1)
                with eng.If(flagged > 0):
                    general[which](eng)

            for choose in (unless_flagged, if_flagged):
                if choose is if_flagged and layer == 0:
                    weigh_risk()
                with nc.Block() as block:
                    @block.sync
                    def _(sp):
                        choose(sp, 0)

                    @block.scalar
                    def _(act):
                        choose(act, 1)

                    @block.tensor
                    def _(pe):
                        choose(pe, 2)

                    @block.vector
                    def _(dve):
                        choose(dve, 3)

        constants()
        for layer, x_in, W_in, a_in, x_to in ((0, x, W0, a0, x_mid), (1, x_mid, W1, a1, out)):
            prepare(layer, x_in, W_in, a_in)
            run_paths(layer, fast_path_0(x_in, x_to) if layer == 0 else fast_path_1(x_in, x_to),
                      general_path(layer, x_in, x_to))


_INS = ['x', 'adj', 'L0_gnn_W', 'L0_gnn_a', 'L1_gnn_W', 'L1_gnn_a']
_OUTS = [((8192, 128), 'float32')]


def kernel(**inputs):
    import numpy as _np
    import concourse.bacc as _bacc
    from concourse import mybir as _mybir
    from concourse.bass_utils import run_bass_kernel_spmd as _run

    nc = _bacc.Bacc("TRN2", target_bir_lowering=False, num_devices=1)
    arrays, args = {}, []
    for name in _INS:
        a = _np.ascontiguousarray(inputs[name])
        arrays[f"in_{name}_dram"] = a
        args.append(nc.dram_tensor(f"in_{name}_dram", a.shape, _mybir.dt.from_np(a.dtype), kind="ExternalInput").ap())
    for i, (shape, dtype) in enumerate(_OUTS):
        dt = _mybir.dt.from_np(_np.dtype(dtype))
        args.append(nc.dram_tensor(f"out_{i}_dram", shape, dt, kind="ExternalOutput").ap())
    kernel_program(nc, *args)
    r = _run(nc, [arrays], core_ids=[0])
    got = tuple(r.results[0][f"out_{i}_dram"] for i in range(len(_OUTS)))
    return got[0]
```

```python
from contextlib import ExitStack

import concourse.bass as bass
from concourse import mybir

ALU = mybir.AluOpType
ACT = mybir.ActivationFunctionType
AX = mybir.AxisListType
F32 = mybir.dt.float32
BF16 = mybir.dt.bfloat16
U8 = mybir.dt.uint8
I32 = mybir.dt.int32

N = 8192
F = 128
P = 128
T = N // P
FZ = F + 1
ALPHA = 0.2
THR = 1e-4
EPS = 1e-5

CH = 2048
NC = N // CH
SLOTS = 2
ADJS = 3
ACCS = 3
UJ = 8
U = T // UJ
UC = U // NC
Q = 16
QT = T // Q
QN = QT * P
XP = 4

UN = 6
LEAD = 4
LOOPS = (T - LEAD) // UN

G0 = 4
GI = G0 * P
NG = T // G0
G1 = 8
CB = CH // P
PAIRS = T // 2
RING = 4
CP = PAIRS // NC
FOLDS = 8

FAST_SPREAD = 85.0
SHIFT = 30.0
MARGIN = 0.01
SMALL = 1e-30
NEVER = 1e30


def kernel_program(nc, x, adj, W0, a0, W1, a1, out):
    ctx = ExitStack()

    def sb(name, shape, dt=F32):
        return ctx.enter_context(nc.sbuf_tensor(name, shape, dt))

    def ps(name, cols):
        return ctx.enter_context(nc.psum_tensor(name, [P, cols], F32))

    sems = {}

    def sem(name):
        if name not in sems:
            sems[name] = ctx.enter_context(nc.semaphore(name))
        return sems[name]

    with ctx:
        arena = sb("arena", [P, 5 * N])

        def part(start, size):
            return arena[:, start:start + size]

        d_row = part(0, N)
        r_row = part(N, N)
        row2 = r_row
        weights = [part((2 + i) * N, N) for i in range(SLOTS)]
        adj_buf = [part(4 * N + i * CH, CH).bitcast(I32) for i in range(ADJS)]
        wT = [part(4 * N + ADJS * CH + i * UJ * P, UJ * P) for i in range(2)]
        h_all = sb("h_all", [P, T, FZ])
        identb = sb("identb", [P, P], BF16)
        ident = sb("ident", [P, P])
        ones = sb("ones", [P, P])
        a_three = sb("a_three", [P, 3])
        mean_row = sb("mean_row", [P, F])
        sd_col = sb("sd_col", [P, T, 3])
        D_col = sb("D_col", [P, T])
        rho_col = sb("rho_col", [P, T])
        r_col = sb("r_col", [P, T])
        low_exp = sb("low_exp", [P, 2])
        at_risk = sb("at_risk", [P, T])
        path = sb("path", [P, 2], I32)
        path_f = sb("path_f", [P, 2])
        lin = sb("lin", [P, T])
        top = sb("top", [P, 1])
        low = sb("low", [P, 1])
        base = sb("base", [P, 1])
        exp_bias = sb("exp_bias", [P, 2])
        flag = sb("flag", [P, 3])
        edges_kept = sb("edges_kept", [P, 1])
        z_part = sb("z_part", [P, SLOTS, NC])
        cnt_part = sb("cnt_part", [P, SLOTS, NC])
        v_part = sb("v_part", [P, NC])
        v_top = sb("v_top", [P, 4])
        neg_m = sb("neg_m", [P, SLOTS])
        z_sum = sb("z_sum", [P, UN])
        n_edges = sb("n_edges", [P, UN])
        theta = sb("theta", [P, UN])
        scale = sb("scale", [P, UN])
        empty = sb("empty", [P, UN])
        x_res = sb("x_res", [P, ACCS, F])
        h_res = sb("h_res", [P, ACCS, F])
        y = sb("y", [P, F])
        y_exp = sb("y_exp", [P, F])
        rest = sb("rest", [P, F])
        x_out = sb("x_out", [P, ACCS, F])

        psum = ps("psum", 8 * 512)

        def bank(i, banks=1):
            return psum[:, i * 512:(i + banks) * 512]

        turn = [bank(0, 2), bank(2, 2)]
        acc = [bank(4 + i) for i in range(ACCS)]
        spare = bank(7)

        x_mid = nc.dram_tensor("x_mid", [N, F], F32, kind="Internal").ap()
        h_mid = nc.dram_tensor("h_mid", [N, F], F32, kind="Internal").ap()
        r_mid = nc.dram_tensor("r_mid", [1, N], F32, kind="Internal").ap()
        d_mid = nc.dram_tensor("d_mid", [1, N], F32, kind="Internal").ap()
        edgesT = nc.dram_tensor("edgesT", [NG * NC, P, CB * GI], U8, kind="Internal").ap()

        assert G0 * CH <= N
        adj_in = [part(i * CH, CH).bitcast(I32) for i in range(G0)]
        adj_in_loaded = [sem(f"adj_in_loaded{i}") for i in range(G0)]
        adj_view = adj.rearrange("(t p) (c n) -> t p c n", p=P, n=CH)

        def constants():
            made = sem("constants_made")
            with nc.Block() as block:
                @block.gpsimd
                def _(pool):
                    nc.gpsimd.memset(ident[:], 0.0).then_inc(made, 1)
                    pool.wait_ge(made, 1)
                    nc.gpsimd.affine_select(out=ident[:], in_=ident[:], compare_op=ALU.not_equal, fill=1.0,
                                            base=0, pattern=[[-1, P]], channel_multiplier=1).then_inc(made, 1)
                    pool.wait_ge(made, 2)
                    nc.gpsimd.tensor_copy(identb[:], ident[:])

                @block.vector
                def _(dve):
                    nc.vector.memset(ones[:], 1.0)
                    nc.vector.memset(a_three[:, 2:3], 1.0)

        def prepare(layer, x_in, W_in, a_in):
            first = layer == 0
            x_all = weights[0].rearrange("p (t f) -> p t f", f=F)
            hn = weights[1].rearrange("p (t f) -> p t f", f=F)
            at = 4 * N
            hnT = [part(at + i * QN, QN) for i in range(2)]
            at += 2 * QN
            st = part(at, 6 * T).rearrange("p (t k) -> p t k", k=6)
            at += 6 * T
            mean, var, std, rstd, tmp, d_valid, invalid = [part(at + i * T, T) for i in range(7)]
            at += 7 * T
            W_ext = part(at, F + 3)
            at += F + 4
            WT = part(at, P)
            at += P
            d_rows, r_rows = [part(at + i * P, P) for i in range(2)]
            at += 2 * P
            mean_cols = part(at, P)
            at += P
            extremes = part(at, 3)
            extreme = part(at + 4, 1)
            extreme_diag = part(at + 8, 3)
            hn_sum = part(at + 12, 1)
            hn_sums = part(at + 16, Q)
            at += 16 + Q
            assert at <= 5 * N

            hn_ps = [bank(i) for i in range(2)]
            h_ps = [bank(2 + 2 * i, 2).rearrange("p (t c) -> p t c", c=256)[:, :, 0:F + 3] for i in range(2)]
            ps_a, ps_b = bank(6), bank(7)

            x_view = x_in.rearrange("(t p) f -> p t f", p=P)
            h_view = h_mid.rearrange("(t p) f -> p t f", p=P)
            n = "prep_"

            def wait(eng, sm, per_layer, value):
                eng.wait_ge(sm, layer * per_layer + value)

            x_loaded = [sem(n + f"x_loaded{i}") for i in range(XP)]
            w_loaded = sem(n + "w_loaded")
            chain = sem(n + f"vector_chain{layer}")
            W_turned = sem(n + "W_turned")
            WT_ready = sem(n + "WT_ready")
            Wa_done = sem(n + "Wa_done")
            W_ext_ready = sem(n + "W_ext_ready")
            var_ready = sem(n + "var_ready")
            std_ready = sem(n + "std_ready")
            hn_ready = sem(n + "hn_ready")
            hn_turned = sem(n + "hn_turned")
            hnT_ready = sem(n + "hnT_ready")
            h_done = sem(n + "h_done")
            h_kept = sem(n + "h_kept")
            extremes_ready = sem(n + "extremes_ready")
            extremes_turned = sem(n + "extremes_turned")
            extreme_ready = sem(n + "extreme_ready")
            extreme_spread = sem(n + "extreme_spread")
            d_valid_ready = sem(n + "d_valid_ready")
            d_turned = sem(n + "d_turned")
            lin_ready = sem(n + "lin_ready")
            r_ready = sem(n + "r_ready")
            r_turned = sem(n + "r_turned")
            rows_ready = sem(n + "rows_ready")
            mean_ready = sem(n + "mean_ready")
            mean_done = sem(n + "mean_done")
            h_stored = sem(n + "h_stored")
            rows_stored = sem(n + "rows_stored")
            TQ = T // XP

            with nc.Block() as block:
                @block.sync
                def _(sp):
                    sp.dma_start(W_ext[:, 0:F], W_in).then_inc(w_loaded, 16)
                    sp.dma_start(a_three[:, 0:1], a_in[0:F, :]).then_inc(w_loaded, 16)
                    sp.dma_start(a_three[:, 1:2], a_in[F:2 * F, :]).then_inc(w_loaded, 16)
                    for i in range(XP):
                        c = slice(i * TQ, (i + 1) * TQ)
                        sp.dma_start(x_all[:, c, :], x_view[:, c, :]).then_inc(x_loaded[i], 16)
                    if first:
                        for k in range(G0):
                            sp.dma_start(adj_in[k], adj_view[k, :, 0, :]).then_inc(adj_in_loaded[k], 16)
                        for q in range(Q):
                            wait(sp, h_kept, 2 * Q, 2 * (q + 1))
                            sp.dma_start(h_view[:, q * QT:(q + 1) * QT, :], h_all[:, q * QT:(q + 1) * QT, 0:F])\
                                .then_inc(h_stored, 16)
                    wait(sp, rows_ready, 2, 1)
                    sp.dma_start(d_mid.rearrange("o (t p) -> (o t) p", p=P), d_rows[0:T, :]).then_inc(rows_stored, 16)
                    wait(sp, rows_ready, 2, 2)
                    sp.dma_start(r_mid.rearrange("o (t p) -> (o t) p", p=P), r_rows[0:T, :]).then_inc(rows_stored, 16)
                    wait(sp, rows_stored, 32, 32)
                    if first:
                        sp.wait_ge(h_stored, 16 * Q)
                        for k in range(G0):
                            sp.wait_ge(adj_in_loaded[k], 16)

                @block.vector
                def _(dve):
                    links = [0]

                    def link(ins):
                        links[0] += 1
                        ins.then_inc(chain, 1)
                        dve.wait_ge(chain, links[0])

                    def variance(i):
                        wait(dve, x_loaded[i], 16, 16)
                        c = slice(i * TQ, (i + 1) * TQ)
                        for t in range(i * TQ, (i + 1) * TQ):
                            last = nc.vector.bn_stats(st[:, t, :], x_all[:, t, :])
                        link(last)
                        nc.vector.tensor_tensor(mean[:, c], st[:, c, 1], st[:, c, 4], ALU.add)
                        nc.vector.tensor_tensor(tmp[:, c], st[:, c, 1], st[:, c, 4], ALU.subtract)
                        link(nc.vector.tensor_tensor(var[:, c], st[:, c, 2], st[:, c, 5], ALU.add))
                        nc.vector.tensor_scalar(mean[:, c], mean[:, c], 0.5, None, ALU.mult)
                        link(nc.vector.tensor_tensor(tmp[:, c], tmp[:, c], tmp[:, c], ALU.mult))
                        link(nc.vector.scalar_tensor_tensor(var[:, c], tmp[:, c], F / 4.0, var[:, c],
                                                            ALU.mult, ALU.add))
                        nc.vector.tensor_scalar(var[:, c], var[:, c], 1.0 / F, EPS, ALU.mult, ALU.add)\
                            .then_inc(var_ready, 1)

                    def inverse(i):
                        c = slice(i * TQ, (i + 1) * TQ)
                        wait(dve, std_ready, XP, i + 1)
                        link(nc.vector.reciprocal(rstd[:, c], std[:, c]))
                        link(nc.vector.tensor_tensor(tmp[:, c], rstd[:, c], rstd[:, c], ALU.mult))
                        link(nc.vector.tensor_tensor(tmp[:, c], tmp[:, c], var[:, c], ALU.mult))
                        link(nc.vector.tensor_scalar(tmp[:, c], tmp[:, c], -0.5, 1.5, ALU.mult, ALU.add))
                        link(nc.vector.tensor_tensor(rstd[:, c], rstd[:, c], tmp[:, c], ALU.mult))

                    def normalise(q):
                        for t in range(q * QT, (q + 1) * QT):
                            last = nc.vector.tensor_scalar(hn[:, t, :], x_all[:, t, :], mean[:, t:t + 1],
                                                           rstd[:, t:t + 1], ALU.subtract, ALU.mult)
                        last.then_inc(hn_ready, 1)

                    wait(dve, W_turned, 1, 1)
                    nc.vector.tensor_copy(WT, ps_a[:, 0:P]).then_inc(WT_ready, 1)
                    wait(dve, Wa_done, 1, 1)
                    nc.vector.tensor_copy(W_ext[:, F:F + 3], ps_b[:, 0:3]).then_inc(W_ext_ready, 1)
                    variance(0)
                    for i in range(XP):
                        if i < XP - 1:
                            variance(i + 1)
                        inverse(i)
                        for q in range(i * Q // XP, (i + 1) * Q // XP):
                            normalise(q)
                    wait(dve, h_kept, 2 * Q, 2 * Q)
                    d = sd_col[:, :, 1]
                    nc.vector.tensor_reduce(extremes[:, 0:1], d, AX.X, ALU.max)
                    if first:
                        nc.vector.tensor_scalar(invalid, sd_col[:, :, 2], 0.0, None, ALU.is_equal)
                    else:
                        nc.vector.tensor_scalar(invalid, d, 0.0, None, ALU.mult)
                    link(nc.vector.tensor_reduce(extremes[:, 1:2], d, AX.X, ALU.min))
                    nc.vector.tensor_scalar(extremes[:, 1:2], extremes[:, 1:2], -1.0, None, ALU.mult)
                    nc.vector.tensor_reduce(extremes[:, 2:3], invalid, AX.X, ALU.max).then_inc(extremes_ready, 1)
                    nc.vector.scalar_tensor_tensor(d_valid, invalid, -NEVER, d, ALU.mult, ALU.add)\
                        .then_inc(d_valid_ready, 1)
                    wait(dve, extremes_turned, 1, 1)
                    link(nc.vector.tensor_reduce(extreme[0:3, :], ps_a[0:3, 0:P], AX.X, ALU.max))
                    nc.vector.tensor_scalar(extreme_diag[0:3, :], ident[0:3, 0:3], extreme[0:3, 0:1], None, ALU.mult)\
                        .then_inc(extreme_ready, 1)
                    wait(dve, extreme_spread, 1, 1)
                    nc.vector.tensor_copy(top[:], ps_b[:, 0:1])
                    nc.vector.tensor_copy(flag[:, 1:2], ps_b[:, 2:3])
                    link(nc.vector.tensor_scalar(low[:], ps_b[:, 1:2], -1.0, None, ALU.mult))
                    nc.vector.tensor_scalar(base[:], low[:], -1.0, None, ALU.add)
                    nc.vector.tensor_scalar(exp_bias[:, 0:1], top[:], -ALPHA, SHIFT, ALU.mult, ALU.add)
                    nc.vector.tensor_scalar(exp_bias[:, 1:2], top[:], ALPHA - 1.0, None, ALU.mult)
                    nc.vector.tensor_scalar(lin[:], sd_col[:, :, 0], top[:, 0:1], 0.0, ALU.add, ALU.max)\
                        .then_inc(lin_ready, 1)
                    wait(dve, d_turned, 1, 1)
                    nc.vector.tensor_copy(d_rows[0:T, :], ps_a[0:T, 0:P]).then_inc(rows_ready, 1)
                    link(nc.vector.tensor_tensor(flag[:, 0:1], top[:], low[:], ALU.subtract))
                    link(nc.vector.tensor_scalar(flag[:, 2:3], flag[:, 0:1], FAST_SPREAD, None, ALU.is_gt))
                    link(nc.vector.tensor_tensor(flag[:, 2:3], flag[:, 2:3], flag[:, 1:2], ALU.max))
                    if first:
                        nc.vector.tensor_copy(edges_kept[:], flag[:, 2:3])
                        link(nc.vector.tensor_copy(path_f[:, 0:1], flag[:, 2:3]))
                    else:
                        link(nc.vector.tensor_tensor(path_f[:, 1:2], flag[:, 2:3], edges_kept[:], ALU.max))
                    nc.vector.tensor_copy(path[:, layer:layer + 1], path_f[:, layer:layer + 1])
                    wait(dve, r_turned, 1, 1)
                    nc.vector.tensor_copy(r_rows[0:T, :], ps_b[0:T, 0:P]).then_inc(rows_ready, 1)
                    if not first:
                        wait(dve, hnT_ready, Q, Q)
                        link(nc.vector.tensor_reduce(hn_sum, hn_sums, AX.X, ALU.add))
                        nc.vector.tensor_scalar(mean_cols, ones[:], hn_sum, 1.0 / N, ALU.mult, ALU.mult)\
                            .then_inc(mean_ready, 1)
                        dve.wait_ge(mean_done, 1)
                        nc.vector.tensor_copy(mean_row[:], hn_ps[0][:, 0:F])

                @block.scalar
                def _(act):
                    def deviation(i):
                        c = slice(i * TQ, (i + 1) * TQ)
                        wait(act, var_ready, XP, i + 1)
                        nc.scalar.activation(std[:, c], var[:, c], ACT.Sqrt).then_inc(std_ready, 1)

                    def keep(q):
                        tiles = slice(q * QT, (q + 1) * QT)
                        wait(act, h_done, Q, q + 1)
                        nc.scalar.activation(h_all[:, tiles, 0:F], h_ps[q % 2][:, :, 0:F], ACT.Identity)\
                            .then_inc(h_kept, 1)
                        nc.scalar.activation(sd_col[:, tiles, :], h_ps[q % 2][:, :, F:F + 3], ACT.Identity)\
                            .then_inc(h_kept, 1)

                    deviation(0)
                    for q in range(Q):
                        if q % (Q // XP) == 0 and q // (Q // XP) < XP - 1:
                            deviation(q // (Q // XP) + 1)
                        wait(act, hn_turned, Q, q + 1)
                        nc.scalar.activation(hnT[q % 2], hn_ps[q % 2], ACT.Relu, accum_out=hn_sums[:, q:q + 1])\
                            .then_inc(hnT_ready, 1)
                        if q >= 1:
                            keep(q - 1)
                    keep(Q - 1)
                    wait(act, lin_ready, 1, 1)
                    nc.scalar.activation(r_col[:], lin[:], ACT.Exp, scale=ALPHA - 1.0).then_inc(r_ready, 1)
                    nc.scalar.activation(D_col[:], sd_col[:, :, 1], ACT.Exp, scale=ALPHA, bias=exp_bias[:, 0:1])
                    nc.scalar.activation(rho_col[:], sd_col[:, :, 1], ACT.Exp, scale=1.0 - ALPHA, bias=exp_bias[:, 1:2])
                    nc.scalar.activation(low_exp[:, 0:1], low[:], ACT.Exp, scale=ALPHA, bias=exp_bias[:, 0:1])
                    nc.scalar.activation(low_exp[:, 1:2], low[:], ACT.Exp, scale=1.0 - ALPHA, bias=exp_bias[:, 1:2])

                @block.tensor
                def _(pe):
                    def turn_hn(q):
                        wait(pe, hn_ready, Q, q + 1)
                        if q >= 2:
                            wait(pe, hnT_ready, Q, q - 1)
                        for i in range(QT):
                            last = nc.tensor.transpose(hn_ps[q % 2][:, i * P:(i + 1) * P], hn[:, q * QT + i, :], ident[:])
                        last.then_inc(hn_turned, 1)

                    def products(q):
                        wait(pe, hnT_ready, Q, q + 1)
                        if q >= 2:
                            wait(pe, h_kept, 2 * Q, 2 * (q - 1))
                        for i in range(QT):
                            last = nc.tensor.matmul(h_ps[q % 2][:, i, :], hnT[q % 2][:, i * P:(i + 1) * P],
                                                    W_ext, start=True, stop=True)
                        last.then_inc(h_done, 1)

                    wait(pe, w_loaded, 48, 48)
                    nc.tensor.transpose(ps_a[:, 0:P], W_ext[:, 0:F], ident[:]).then_inc(W_turned, 1)
                    wait(pe, WT_ready, 1, 1)
                    nc.tensor.matmul(ps_b[:, 0:3], WT, a_three[:], start=True, stop=True).then_inc(Wa_done, 1)
                    turn_hn(0)
                    wait(pe, W_ext_ready, 1, 1)
                    for q in range(Q):
                        if q + 1 < Q:
                            turn_hn(q + 1)
                        products(q)
                    wait(pe, extremes_ready, 1, 1)
                    nc.tensor.transpose(ps_a[0:3, 0:P], extremes, ident[:]).then_inc(extremes_turned, 1)
                    wait(pe, extreme_ready, 1, 1)
                    nc.tensor.matmul(ps_b[:, 0:3], ones[0:3, :], extreme_diag[0:3, :], start=True, stop=True)\
                        .then_inc(extreme_spread, 1)
                    wait(pe, d_valid_ready, 1, 1)
                    nc.tensor.transpose(ps_a[0:T, 0:P], d_valid, ident[:]).then_inc(d_turned, 1)
                    wait(pe, lin_ready, 1, 1)
                    wait(pe, r_ready, 1, 1)
                    nc.tensor.transpose(ps_b[0:T, 0:P], r_col[:], ident[:]).then_inc(r_turned, 1)
                    if not first:
                        pe.wait_ge(mean_ready, 1)
                        nc.tensor.matmul(hn_ps[0][:, 0:F], mean_cols, W_ext[:, 0:F], start=True, stop=True)\
                            .then_inc(mean_done, 1)

        def general_path(layer, x_in, x_to):
            first = layer == 0
            n = f"g{layer}_"
            d_loaded = sem(n + "d_loaded")
            h_restored = sem(n + "h_restored")
            LK = 2 * NC
            adj_loaded = [sem(n + f"adj_loaded{i}") for i in range(ADJS)]
            row_link = sem(n + "row_link")
            adj_used = sem(n + "adj_used")
            probe_link = sem(n + "probe_link")
            probed = sem(n + "chunk_probed")
            m_ready = sem(n + "m_ready")
            lrelu_link = sem(n + "lrelu_link")
            lrelu_done = sem(n + "lrelu_done")
            e_ready = sem(n + "e_ready")
            thresholded = sem(n + "thresholded")
            turned = sem(n + "unit_turned")
            by_act = sem(n + "wT_by_act")
            summed = sem(n + "unit_summed")
            acc_read = sem(n + "acc_read")
            y_neg_ready = sem(n + "y_neg_ready")
            y_exp_ready = sem(n + "y_exp_ready")
            rest_link = sem(n + "rest_link")
            res_loaded = [sem(n + f"res_loaded{i}") for i in range(ACCS)]
            out_ready = sem(n + "out_ready")
            stored = [sem(n + f"stored{i}") for i in range(ACCS)]
            tile_link = sem(n + "tile_link")
            finish_link = sem(n + "finish_link")
            SHIFT_LINKS = 4
            TILE_LINKS = SHIFT_LINKS + (3 if first else 1)
            FINISH_LINKS = 3
            RES = 32 if first else 16

            x_view = x_in.rearrange("(t p) f -> t p f", p=P)
            h_view = h_mid.rearrange("(t p) f -> t p f", p=P)
            out_view = x_to.rearrange("(t p) f -> t p f", p=P)
            adj_view = adj.rearrange("(t p) (c n) -> t p c n", p=P, n=CH)

            def chunk(c):
                return slice(c * CH, (c + 1) * CH)

            def steps(eng, step):
                for st in range(LEAD):
                    step(0, st)
                with eng.Fori(0, LOOPS) as it:
                    for r in range(UN):
                        step(it, LEAD + r)
                for st in range(LEAD + LOOPS * UN, T + 3):
                    step(0, st)

            def wait(eng, sm, it, per_step, value):
                if value > 0:
                    eng.wait_ge(sm, it * (UN * per_step) + value)

            def runs(st, lag):
                return 0 <= st - lag < T

            def wait_adj(eng, it, st, i):
                no = st * LK + i
                eng.wait_ge(adj_loaded[no % ADJS], it * (UN * LK // ADJS * 16) + (no // ADJS + 1) * 16)

            def wait_slot(eng, it, st, c):
                wait(eng, turned, it, U, (st - SLOTS) * U + (c + 1) * UC if st >= SLOTS else 0)

            def wait_moved(eng, it, st, u):
                if u < 0:
                    st, u = st - 1, u + U
                wait(eng, by_act, it, U, (st - 1) * U + u + 1 if st >= 1 else 0)

            def sync_rows(sp):
                def step(it, st):
                    for i in range(LK):
                        if runs(st, 0):
                            no = st * LK + i
                            wait(sp, adj_used, it, LK, no - ADJS + 1)
                            sp.dma_start(adj_buf[no % ADJS], adj_view[it * UN + st, :, i % NC, :])\
                                .then_inc(adj_loaded[no % ADJS], 16)
                        if i == 2 and runs(st, 3):
                            b = (st - 3) % ACCS
                            wait(sp, out_ready, it, 1, st - 2)
                            sp.dma_start(out_view[it * UN + (st - 3)], x_out[:, b]).then_inc(stored[b], 16)
                        if i == 3 and runs(st, 1):
                            b = (st - 1) % ACCS
                            wait(sp, out_ready, it, 1, st - ACCS)
                            sp.dma_start(x_res[:, b], x_view[it * UN + (st - 1)]).then_inc(res_loaded[b], 16)
                            if first:
                                sp.dma_start(h_res[:, b], h_view[it * UN + (st - 1)]).then_inc(res_loaded[b], 16)

                sp.dma_start(d_row, d_mid.partition_broadcast(P)).then_inc(d_loaded, 16)
                if first:
                    sp.dma_start(h_all[:, :, 0:F], h_mid.rearrange("(t p) f -> p t f", p=P)).then_inc(h_restored, 16)
                steps(sp, step)
                for b in range(ACCS):
                    sp.wait_ge(stored[b], 16 * len(range(b, T, ACCS)))

            def scalar_rows(act):
                def move_unit(it, st, u):
                    if runs(st, 1):
                        wait(act, turned, it, U, (st - 1) * U + u + 1)
                        wait(act, summed, it, U, (st - 1) * U + u - 1)
                        nc.scalar.activation(wT[u % 2], turn[u % 2], ACT.Identity)\
                            .then_inc(by_act, 1)

                def step(it, st):
                    for c in range(NC):
                        for u in range(c * UC, (c + 1) * UC):
                            move_unit(it, st, u)
                        if first and c == 1 and runs(st, 2):
                            wait(act, acc_read, it, 1, st - 1)
                            wait(act, rest_link, it, 2, (st - 3) * 2 + 1)
                            nc.scalar.activation(y_exp[:], y[:], ACT.Relu, scale=-1.0).then_inc(y_neg_ready, 1)
                            wait(act, y_neg_ready, it, 1, st - 1)
                            nc.scalar.activation(y_exp[:], y_exp[:], ACT.Exp, scale=-1.0).then_inc(y_exp_ready, 1)
                    if runs(st, 0):
                        wait(act, m_ready, it, 1, st + 1)
                        for c in range(NC):
                            w = weights[st % SLOTS][:, chunk(c)]
                            wait(act, lrelu_done, it, NC, st * NC + c + 1)
                            nc.scalar.activation(w, w, ACT.Exp, bias=neg_m[:, st % SLOTS:st % SLOTS + 1])\
                                .then_inc(e_ready, 1)

                steps(act, step)

            def tensor_rows(pe):
                def turn_unit(it, st, u):
                    if u % UC == 0:
                        c = u // UC
                        if first:
                            wait(pe, thresholded, it, NC, (st - 1) * NC + c + 1)
                        else:
                            wait(pe, adj_used, it, LK, (st - 1) * LK + LK - NC + c + 1)
                    wait_moved(pe, it, st, u - 2)
                    for b in range(UJ):
                        j = (u * UJ + b) * P
                        last = nc.tensor.transpose(turn[u % 2][:, b * P:(b + 1) * P],
                                                   weights[(st - 1) % SLOTS][:, j:j + P], ident[:])
                    last.then_inc(turned, 1)

                def sum_unit(it, st, u):
                    wait_moved(pe, it, st, u)
                    if u == 0:
                        wait(pe, acc_read, it, 1, st - ACCS)
                    for b in range(UJ):
                        j = u * UJ + b
                        last = nc.tensor.matmul(acc[(st - 1) % ACCS][:, 0:F], wT[u % 2][:, b * P:(b + 1) * P],
                                                h_all[:, j, 0:F], start=(j == 0), stop=(j == T - 1))
                    last.then_inc(summed, 1)

                def step(it, st):
                    if runs(st, 1):
                        for u in range(U + 1):
                            if u < U:
                                turn_unit(it, st, u)
                            if u >= 1:
                                sum_unit(it, st, u - 1)

                if first:
                    pe.wait_ge(h_restored, 16)
                steps(pe, step)

            def vector_rows(dve):
                def link(ins, sm, it, per_step, value):
                    ins.then_inc(sm, 1)
                    wait(dve, sm, it, per_step, value)

                def tlink(ins, it, st, i):
                    link(ins, tile_link, it, TILE_LINKS, st * TILE_LINKS + i)

                def flink(ins, it, st, i):
                    link(ins, finish_link, it, FINISH_LINKS, (st - 2) * FINISH_LINKS + i)

                def probe(it, st, c):
                    w = weights[st % SLOTS][:, chunk(c)]
                    wait_adj(dve, it, st, c)
                    wait_slot(dve, it, st, c)
                    nc.vector.scalar_tensor_tensor(w, adj_buf[(st * LK + c) % ADJS], 0.0, row2[:, chunk(c)],
                                                   ALU.is_gt, ALU.mult).then_inc(adj_used, 1)
                    wait(dve, adj_used, it, LK, st * LK + c + 1)
                    nc.vector.tensor_reduce(v_part[:, c:c + 1], w, AX.X, ALU.max).then_inc(probe_link, 1)
                    wait(dve, probe_link, it, NC, st * NC + c + 1)
                    nc.vector.tensor_scalar(w, w, 0.0, None, ALU.is_gt, ALU.add,
                                            accum_out=cnt_part[:, st % SLOTS, c:c + 1]).then_inc(probed, 1)

                def shift(it, st):
                    wait(dve, probed, it, NC, (st + 1) * NC)
                    tlink(nc.vector.tensor_reduce(v_top[:, 0:1], v_part[:], AX.X, ALU.max), it, st, 1)
                    tlink(nc.vector.tensor_scalar(v_top[:, 1:2], v_top[:, 0:1], base[:, 0:1], None, ALU.add),
                          it, st, 2)
                    tlink(nc.vector.tensor_tensor(v_top[:, 2:3], v_top[:, 1:2],
                                                  sd_col[:, bass.ds(it * UN + st, 1), 0], ALU.add), it, st, 3)
                    tlink(nc.vector.scalar_tensor_tensor(v_top[:, 3:4], v_top[:, 2:3], ALPHA, v_top[:, 2:3],
                                                         ALU.mult, ALU.max), it, st, 4)
                    nc.vector.tensor_scalar(neg_m[:, st % SLOTS:st % SLOTS + 1], v_top[:, 3:4], -1.0, -MARGIN,
                                            ALU.mult, ALU.add).then_inc(m_ready, 1)

                def lrelu(it, st, c):
                    w = weights[st % SLOTS][:, chunk(c)]
                    nc.vector.tensor_scalar(w, d_row[:, chunk(c)], sd_col[:, bass.ds(it * UN + st, 1), 0], None,
                                            ALU.add).then_inc(lrelu_link, 1)
                    wait(dve, lrelu_link, it, NC, st * NC + c + 1)
                    nc.vector.scalar_tensor_tensor(w, w, ALPHA, w, ALU.mult, ALU.max).then_inc(lrelu_done, 1)

                def mask(it, st, c):
                    w = weights[st % SLOTS][:, chunk(c)]
                    wait_adj(dve, it, st, NC + c)
                    wait(dve, e_ready, it, NC, st * NC + c + 1)
                    nc.vector.scalar_tensor_tensor(w, adj_buf[(st * LK + NC + c) % ADJS], 0.0, w, ALU.max, ALU.min,
                                                   accum_out=z_part[:, st % SLOTS, c:c + 1]).then_inc(adj_used, 1)

                def row_sums(it, st):
                    b = slice(st % UN, st % UN + 1)
                    wait(dve, adj_used, it, LK, (st + 1) * LK)
                    if first:
                        tlink(nc.vector.tensor_reduce(n_edges[:, b], cnt_part[:, st % SLOTS, :], AX.X, ALU.add),
                              it, st, SHIFT_LINKS + 1)
                    ins = nc.vector.tensor_reduce(z_sum[:, b], z_part[:, st % SLOTS, :], AX.X, ALU.add)
                    if first:
                        tlink(ins, it, st, SHIFT_LINKS + 2)
                        tlink(nc.vector.tensor_scalar(theta[:, b], z_sum[:, b], THR, None, ALU.mult),
                              it, st, SHIFT_LINKS + 3)
                    else:
                        tlink(ins, it, st, SHIFT_LINKS + 1)

                def threshold(it, st, c):
                    w = weights[st % SLOTS][:, chunk(c)]
                    nc.vector.scalar_tensor_tensor(w, w, theta[:, st % UN:st % UN + 1], w, ALU.is_ge, ALU.mult)\
                        .then_inc(thresholded, 1)

                def finish(it, st):
                    g = st - 2
                    a = acc[g % ACCS]
                    b = slice(g % UN, g % UN + 1)
                    z = z_sum[:, b]
                    wait(dve, summed, it, U, (g + 1) * U)
                    flink(nc.vector.tensor_scalar(scale[:, b], z, SMALL, None, ALU.max), it, st, 1)
                    flink(nc.vector.reciprocal(scale[:, b], scale[:, b]), it, st, 2)
                    no = g // ACCS
                    dve.wait_ge(res_loaded[g % ACCS], it * (UN // ACCS * RES) + (no + 1) * RES)
                    if first:
                        flink(nc.vector.tensor_tensor(scale[:, b], scale[:, b], n_edges[:, b], ALU.mult), it, st, 3)
                        wait(dve, y_exp_ready, it, 1, g)
                        nc.vector.scalar_tensor_tensor(y[:], a[:, 0:F], scale[:, b], h_res[:, g % ACCS],
                                                       ALU.mult, ALU.add).then_inc(acc_read, 1)
                        return
                    if no >= 1:
                        dve.wait_ge(stored[g % ACCS], it * (UN // ACCS * 16) + no * 16)
                    flink(nc.vector.tensor_scalar(empty[:, b], z, 0.0, None, ALU.is_le), it, st, 3)
                    nc.vector.scalar_tensor_tensor(x_out[:, g % ACCS], a[:, 0:F], scale[:, b], x_res[:, g % ACCS],
                                                   ALU.mult, ALU.add).then_inc(acc_read, 1)
                    wait(dve, acc_read, it, 1, g + 1)
                    nc.vector.scalar_tensor_tensor(x_out[:, g % ACCS], mean_row[:], empty[:, b], x_out[:, g % ACCS],
                                                   ALU.mult, ALU.add).then_inc(out_ready, 1)

                def finish_elu(it, st):
                    g = st - 2
                    wait(dve, y_exp_ready, it, 1, g + 1)
                    link(nc.vector.tensor_scalar(rest[:], y_exp[:], -1.0, None, ALU.add),
                         rest_link, it, 2, g * 2 + 1)
                    if g >= ACCS:
                        dve.wait_ge(stored[g % ACCS], it * (UN // ACCS * 16) + g // ACCS * 16)
                    link(nc.vector.scalar_tensor_tensor(rest[:], y[:], 0.0, rest[:], ALU.max, ALU.add),
                         rest_link, it, 2, g * 2 + 2)
                    nc.vector.tensor_tensor(x_out[:, g % ACCS], rest[:], x_res[:, g % ACCS], ALU.add)\
                        .then_inc(out_ready, 1)

                def step(it, st):
                    makes, finishes = runs(st, 0), runs(st, 2)
                    if finishes:
                        finish(it, st)
                    if makes:
                        for c in range(NC):
                            probe(it, st, c)
                        shift(it, st)
                        for c in range(NC):
                            lrelu(it, st, c)
                        for c in range(NC):
                            mask(it, st, c)
                        row_sums(it, st)
                        if first:
                            for c in range(NC):
                                threshold(it, st, c)
                    if first and finishes:
                        finish_elu(it, st)

                dve.wait_ge(d_loaded, 16)
                nc.vector.tensor_scalar(row2, d_row, base[:, 0:1], 0.0, ALU.subtract, ALU.max).then_inc(row_link, 1)
                dve.wait_ge(row_link, 1)
                steps(dve, step)

            return sync_rows, scalar_rows, tensor_rows, vector_rows


        def wait_in(eng, sm, it, per_group, value):
            if value > 0:
                eng.wait_ge(sm, it * (2 * per_group) + value)

        def groups_of(eng, groups, group):
            group(0, 0)
            group(0, 1)
            with eng.Fori(0, (groups - 4) // 2) as it:
                group(it, 2)
                group(it, 3)
            group(0, groups - 2)
            group(0, groups - 1)

        def acc_tile(group, tiles, k):
            first_bank = (4 if tiles == G0 else 0) + group % 2 * (tiles // 2)
            b = bank(first_bank + k // 2)
            return b[:, k % 2 * 256:k % 2 * 256 + FZ]

        def load_r(sp, r_loaded, i):
            c = slice(0, G0 * P) if i == 0 else slice(G0 * P, G1 * P) if i == 1 else slice(G1 * P, N)
            sp.dma_start(r_row[:, c], r_mid[:, c].partition_broadcast(P)).then_inc(r_loaded[i], 16)

        def fold(h_folded, i):
            D = D_col[:].rearrange("p (t o) -> p t o", o=1)
            if i == 0:
                nc.vector.tensor_copy(h_all[:, :, F:FZ], D)
            c = slice(i * T // FOLDS, (i + 1) * T // FOLDS)
            nc.vector.tensor_tensor(h_all[:, c, 0:F], h_all[:, c, 0:F], D[:, c].to_broadcast([P, T // FOLDS, F]),
                                    ALU.mult).then_inc(h_folded, 1)

        def fast_path_0(x_in, x_to):
            n = "f0_"
            h_folded = sem(n + "h_folded")
            r_loaded = [sem(n + f"r_loaded{i}") for i in range(3)]
            masked = sem(n + "masked")
            counted = sem(n + "counted")
            turned = sem(n + "turned")
            formed = sem(n + "formed")
            copied = sem(n + "copied")
            summed = sem(n + "summed")
            edges_stored = [sem(n + f"edges_stored{i}") for i in range(2)]
            counts_read = sem(n + "counts_read")
            acc_read = sem(n + "acc_read")
            y_neg_ready = sem(n + "y_neg_ready")
            y_exp_ready = sem(n + "y_exp_ready")
            res_loaded = sem(n + "res_loaded")
            out_ready = sem(n + "out_ready")
            stored = sem(n + "stored")
            chain = sem(n + "finish_chain")
            LINKS = 7

            at = 2 * N
            edges = [part(at + i * GI * CB // 2, GI * CB // 2).bitcast(BF16).rearrange("p (t c) -> p t c", t=G0)
                     for i in range(2)]
            at += GI * CB
            wTs = [part(at + i * 2 * GI, 2 * GI) for i in range(RING)]
            at += RING * 2 * GI
            edge_out = [part(at + i * CB * GI // 4, CB * GI // 4).bitcast(U8) for i in range(2)]
            at += CB * GI // 2
            copies = part(at, CH // 2).bitcast(BF16)
            at += CH // 2
            cnt = [part(at + i * G0 * NC, G0 * NC).rearrange("p (t c) -> p t c", c=NC) for i in range(2)]
            at += 2 * G0 * NC
            ne, zs, fl = [part(at + i * G0, G0) for i in range(3)]
            at += 3 * G0
            xr, hr, yy, ye, xo = [part(at + i * GI, GI) for i in range(5)]
            at += 5 * GI
            assert at <= 5 * N
            edge_ps = [bank(i).bitcast(BF16) for i in range(RING)]

            x_view = x_in.rearrange("(g t p) f -> g p t f", p=P, t=G0)
            h_view = h_mid.rearrange("(g t p) f -> g p t f", p=P, t=G0)
            out_view = x_to.rearrange("(g t p) f -> g p t f", p=P, t=G0)

            def sync_rows(sp):
                def group(it, g):
                    for c in range(NC):
                        for k in range(G0):
                            if g == 0 and c == 0:
                                continue
                            u = g * NC + c
                            wait_in(sp, masked, it, NC * G0, (u - 1) * G0 + k + 1)
                            sp.dma_start(adj_in[k], adj_view[it * (2 * G0) + (g * G0 + k), :, c, :])\
                                .then_inc(adj_in_loaded[k], 16)
                        if g == 0 and c == 1:
                            load_r(sp, r_loaded, 1)
                            load_r(sp, r_loaded, 2)
                        if g * NC + c >= 2:
                            store_edges(it, g, c - 2)
                        if c == 2:
                            if g >= 1:
                                wait_in(sp, out_ready, it, 1, g)
                                sp.dma_start(out_view[it * 2 + (g - 1)], xo.rearrange("p (t f) -> p t f", t=G0))\
                                    .then_inc(stored, 16)
                            sp.dma_start(xr.rearrange("p (t f) -> p t f", t=G0), x_view[it * 2 + g])\
                                .then_inc(res_loaded, 16)
                            sp.dma_start(hr.rearrange("p (t f) -> p t f", t=G0), h_view[it * 2 + g])\
                                .then_inc(res_loaded, 16)

                def store_edges(it, g, c):
                    if c < 0:
                        g, c = g - 1, c + NC
                    wait_in(sp, copied, it, PAIRS, g * PAIRS + (c + 1) * CP)
                    sp.dma_start(edgesT[it * (2 * NC) + (g * NC + c)], edge_out[c % 2]).then_inc(edges_stored[c % 2], 16)

                load_r(sp, r_loaded, 0)
                groups_of(sp, NG, group)
                store_edges(0, NG - 1, NC - 2)
                store_edges(0, NG - 1, NC - 1)
                sp.wait_ge(out_ready, NG)
                sp.dma_start(out_view[NG - 1], xo.rearrange("p (t f) -> p t f", t=G0)).then_inc(stored, 16)
                sp.wait_ge(stored, 16 * NG)
                for i in range(2):
                    sp.wait_ge(edges_stored[i], 16 * NG * NC // 2)

            def scalar_rows(act):
                def count(it, g, c, k):
                    if c >= NC:
                        g, c = g + 1, c - NC
                    if g >= NG:
                        return
                    u = g * NC + c
                    wait_in(act, masked, it, NC * G0, u * G0 + k + 1)
                    wait_in(act, counted, it, NC * G0, u * G0 + k)
                    if c == 0 and k == 0:
                        wait_in(act, counts_read, it, 1, g - 1)
                    nc.scalar.activation(copies, edges[c % 2][:, k, :], ACT.Identity,
                                         accum_out=cnt[g % 2][:, k, c:c + 1]).then_inc(counted, 1)

                def group(it, g):
                    for p in range(PAIRS):
                        c, q = p // CP, p % CP
                        m = g * PAIRS + p
                        wait_in(act, formed, it, 2 * PAIRS, 2 * (m + 1))
                        if q == 0 and g * NC + c >= 2:
                            act.wait_ge(edges_stored[c % 2], it * (NC * 16) + (g * NC + c) // 2 * 16)
                        nc.scalar.activation(edge_out[c % 2][:, q * 2 * GI:(q + 1) * 2 * GI], edge_ps[m % RING],
                                             ACT.Identity).then_inc(copied, 1)
                        if q < G0:
                            count(it, g, c + 1, q)
                        if p == 9 and g >= 1:
                            elu(it, g - 1)

                def elu(it, g):
                    wait_in(act, acc_read, it, 1, g + 1)
                    nc.scalar.activation(ye, yy, ACT.Relu, scale=-1.0).then_inc(y_neg_ready, 1)
                    wait_in(act, y_neg_ready, it, 1, g + 1)
                    nc.scalar.activation(ye, ye, ACT.Exp, scale=-1.0).then_inc(y_exp_ready, 1)

                for k in range(G0):
                    count(0, 0, 0, k)
                groups_of(act, NG, group)
                elu(0, NG - 1)

            def tensor_rows(pe):
                def turn_pair(it, g, p):
                    if p >= PAIRS:
                        g, p = g + 1, p - PAIRS
                    if g >= NG:
                        return
                    c, q = p // CP, p % CP
                    m = g * PAIRS + p
                    if q == 0:
                        wait_in(pe, masked, it, NC * G0, (g * NC + c + 1) * G0)
                    wait_in(pe, copied, it, PAIRS, m - RING + 1)
                    for b in range(2):
                        for k in range(G0):
                            last = nc.tensor.transpose(edge_ps[m % RING][:, (b * G0 + k) * P:(b * G0 + k + 1) * P],
                                                       edges[c % 2][:, k, (2 * q + b) * P:(2 * q + b + 1) * P],
                                                       identb[:])
                    last.then_inc(turned, 1)

                def sum_pair(it, g, p):
                    m = g * PAIRS + p
                    if p == 0:
                        wait_in(pe, acc_read, it, 1, g - 1)
                    for b in range(2):
                        j = 2 * p + b
                        if g == 0 and j % (T // FOLDS) == 0:
                            pe.wait_ge(h_folded, j // (T // FOLDS) + 1)
                        wait_in(pe, formed, it, 2 * PAIRS, m * 2 + b + 1)
                        for k in range(G0):
                            last = nc.tensor.matmul(acc_tile(g, G0, k),
                                                    wTs[m % RING][:, b * GI + k * P:b * GI + (k + 1) * P],
                                                    h_all[:, j, :], start=(j == 0 and k % 2 == 0), stop=(j == T - 1),
                                                    skip_group_check=True)
                    last.then_inc(summed, 1)

                def group(it, g):
                    for p in range(PAIRS):
                        turn_pair(it, g, p + 2)
                        sum_pair(it, g, p)

                turn_pair(0, 0, 0)
                turn_pair(0, 0, 1)
                groups_of(pe, NG, group)

            def vector_rows(dve):
                def mark(it, g, c, k):
                    if c >= NC:
                        g, c = g + 1, c - NC
                    if g >= NG:
                        return
                    u = g * NC + c
                    dve.wait_ge(adj_in_loaded[k], it * (2 * NC * 16) + (u + 1) * 16)
                    wait_in(dve, turned, it, PAIRS, (u - 1) * CP)
                    wait_in(dve, counted, it, NC * G0, (u - 2) * G0 + k + 1)
                    nc.vector.tensor_scalar(edges[c % 2][:, k, :], adj_in[k], 0.0, None, ALU.is_gt).then_inc(masked, 1)

                def form(it, g, p):
                    m = g * PAIRS + p
                    wait_in(dve, turned, it, PAIRS, m + 1)
                    wait_in(dve, summed, it, PAIRS, m - RING + 1)
                    for b in range(2):
                        nc.vector.scalar_tensor_tensor(wTs[m % RING][:, b * GI:(b + 1) * GI],
                                                       r_row[:, bass.ds(it * (2 * GI) + g * GI, GI)],
                                                       rho_col[:, 2 * p + b:2 * p + b + 1],
                                                       edge_ps[m % RING][:, b * GI:(b + 1) * GI],
                                                       ALU.max, ALU.mult).then_inc(formed, 1)

                def link(ins, it, g, i):
                    ins.then_inc(chain, 1)
                    wait_in(dve, chain, it, LINKS, g * LINKS + i)

                def finish(it, g):
                    four = bass.ds(it * (2 * G0) + g * G0, G0)
                    wait_in(dve, summed, it, PAIRS, (g + 1) * PAIRS)
                    wait_in(dve, counted, it, NC * G0, (g + 1) * NC * G0)
                    nc.vector.tensor_reduce(ne, cnt[g % 2], AX.X, ALU.add).then_inc(counts_read, 1)
                    for k in range(G0):
                        last = nc.vector.tensor_copy(zs[:, k:k + 1], acc_tile(g, G0, k)[:, F:FZ])
                    link(last, it, g, 1)
                    link(nc.vector.tensor_scalar(fl, r_col[:, four], low_exp[:, 1:2], low_exp[:, 0:1],
                                                 ALU.max, ALU.mult), it, g, 2)
                    nc.vector.scalar_tensor_tensor(at_risk[:, four], zs, THR * 1.001, fl, ALU.mult, ALU.is_gt)
                    link(nc.vector.tensor_scalar(zs, zs, SMALL, None, ALU.max), it, g, 3)
                    link(nc.vector.reciprocal(zs, zs), it, g, 4)
                    wait_in(dve, counts_read, it, 1, g + 1)
                    link(nc.vector.tensor_tensor(zs, zs, ne, ALU.mult), it, g, 5)
                    dve.wait_ge(res_loaded, it * 64 + (g + 1) * 32)
                    for k in range(G0):
                        cols = slice(k * F, (k + 1) * F)
                        last = nc.vector.scalar_tensor_tensor(yy[:, cols], acc_tile(g, G0, k)[:, 0:F], zs[:, k:k + 1],
                                                              hr[:, cols], ALU.mult, ALU.add)
                    last.then_inc(acc_read, 1)

                def finish_elu(it, g):
                    wait_in(dve, y_exp_ready, it, 1, g + 1)
                    link(nc.vector.tensor_scalar(ye, ye, -1.0, None, ALU.add), it, g, 6)
                    link(nc.vector.scalar_tensor_tensor(ye, yy, 0.0, ye, ALU.max, ALU.add), it, g, 7)
                    if g >= 1:
                        dve.wait_ge(stored, it * 32 + g * 16)
                    nc.vector.tensor_tensor(xo, ye, xr, ALU.add).then_inc(out_ready, 1)

                def group(it, g):
                    if g == 1:
                        dve.wait_ge(r_loaded[1], 16)
                        dve.wait_ge(r_loaded[2], 16)
                    for p in range(PAIRS):
                        c, q = p // CP, p % CP
                        form(it, g, p)
                        if g == 0 and p % (PAIRS // FOLDS) == 0 and p < PAIRS - PAIRS // FOLDS:
                            fold(h_folded, p // (PAIRS // FOLDS) + 1)
                        if q < G0:
                            mark(it, g, c + 1, q)
                        if p == 5 and g >= 1:
                            finish(it, g - 1)
                        if p == 11 and g >= 1:
                            finish_elu(it, g - 1)

                fold(h_folded, 0)
                for k in range(G0):
                    mark(0, 0, 0, k)
                dve.wait_ge(r_loaded[0], 16)
                groups_of(dve, NG, group)
                finish(0, NG - 1)
                finish_elu(0, NG - 1)
                dve.wait_ge(out_ready, NG)
                nc.vector.tensor_reduce(flag[:, 0:1], at_risk[:], AX.X, ALU.max)

            return sync_rows, scalar_rows, tensor_rows, vector_rows

        def weigh_risk():
            ready, counted = sem("risk_counted"), sem("risk_flagged")
            with nc.Block() as block:
                @block.tensor
                def _(pe):
                    nc.tensor.matmul(spare[:, 0:1], ones[:], flag[:, 0:1], start=True, stop=True).then_inc(ready, 1)

                @block.vector
                def _(dve):
                    dve.wait_ge(ready, 1)
                    nc.vector.tensor_scalar(flag[:, 1:2], spare[:, 0:1], 0.0, None, ALU.is_gt).then_inc(counted, 1)
                    dve.wait_ge(counted, 1)
                    nc.vector.tensor_tensor(path_f[:, 0:1], edges_kept[:], flag[:, 1:2], ALU.max).then_inc(counted, 1)
                    dve.wait_ge(counted, 2)
                    nc.vector.tensor_copy(path[:, 0:1], path_f[:, 0:1])

        def fast_path_1(x_in, x_to):
            n = "f1_"
            NG1 = T // G1
            R1 = G1 * P
            h_folded = sem(n + "h_folded")
            r_loaded = [sem(n + f"r_loaded{i}") for i in range(3)]
            edges_loaded = [sem(n + f"edges_loaded{i}") for i in range(2)]
            formed = sem(n + "formed")
            summed = sem(n + "summed")
            acc_read = sem(n + "acc_read")
            res_loaded = sem(n + "res_loaded")
            stored = sem(n + "stored")
            chain = sem(n + "finish_chain")
            LINKS = 5

            at = 2 * N
            edges = [part(at + i * CB * R1 // 4, CB * R1 // 4).bitcast(U8)
                     .rearrange("p (h b i) -> p h b i", h=2, b=CB) for i in range(2)]
            at += CB * R1 // 2
            wTs = [part(at + i * R1, R1) for i in range(RING)]
            at += RING * R1
            zs, em = [part(at + i * G1, G1) for i in range(2)]
            at += 2 * G1
            xr, xo = [part(at + i * G1 * F, G1 * F) for i in range(2)]
            at += 2 * G1 * F
            assert at <= 5 * N

            x_view = x_in.rearrange("(g t p) f -> g p t f", p=P, t=G1)
            out_view = x_to.rearrange("(g t p) f -> g p t f", p=P, t=G1)

            def sync_rows(sp):
                def group(it, g):
                    for c in range(NC):
                        u = g * NC + c
                        wait_in(sp, formed, it, T, (u - 1) * CB)
                        for h in range(2):
                            sp.dma_start(edges[c % 2][:, h].rearrange("p b i -> p (b i)"),
                                         edgesT[it * (4 * NC) + ((2 * g + h) * NC + c)]).then_inc(edges_loaded[c % 2], 16)
                        if g == 0 and c == 1:
                            load_r(sp, r_loaded, 2)
                        if c == 2:
                            if g >= 1:
                                wait_in(sp, acc_read, it, 1, g)
                                sp.dma_start(out_view[it * 2 + (g - 1)], xo.rearrange("p (t f) -> p t f", t=G1))\
                                    .then_inc(stored, 16)
                            sp.dma_start(xr.rearrange("p (t f) -> p t f", t=G1), x_view[it * 2 + g])\
                                .then_inc(res_loaded, 16)

                load_r(sp, r_loaded, 0)
                load_r(sp, r_loaded, 1)
                groups_of(sp, NG1, group)
                sp.wait_ge(acc_read, NG1)
                sp.dma_start(out_view[NG1 - 1], xo.rearrange("p (t f) -> p t f", t=G1)).then_inc(stored, 16)
                sp.wait_ge(stored, 16 * NG1)

            def scalar_rows(act):
                pass

            def tensor_rows(pe):
                def group(it, g):
                    for j in range(T):
                        m = g * T + j
                        if j == 0:
                            wait_in(pe, acc_read, it, 1, g - 1)
                        if g == 0 and j % (T // FOLDS) == 0:
                            pe.wait_ge(h_folded, j // (T // FOLDS) + 1)
                        wait_in(pe, formed, it, T, m + 1)
                        for k in range(G1):
                            last = nc.tensor.matmul(acc_tile(g, G1, k), wTs[m % RING][:, k * P:(k + 1) * P],
                                                    h_all[:, j, :], start=(j == 0 and k % 2 == 0), stop=(j == T - 1),
                                                    skip_group_check=True)
                        last.then_inc(summed, 1)

                groups_of(pe, NG1, group)

            def vector_rows(dve):
                def form(it, g, j):
                    m = g * T + j
                    c, b = j // CB, j % CB
                    if b == 0:
                        u = g * NC + c
                        dve.wait_ge(edges_loaded[c % 2], it * (NC * 32) + (u // 2 + 1) * 32)
                    wait_in(dve, summed, it, T, m - RING + 1)
                    nc.vector.scalar_tensor_tensor(wTs[m % RING].rearrange("p (h i) -> p h i", h=2),
                                                   r_row[:, bass.ds(it * (2 * R1) + g * R1, R1)]
                                                   .rearrange("p (h i) -> p h i", h=2),
                                                   rho_col[:, j:j + 1], edges[c % 2][:, :, b, :],
                                                   ALU.max, ALU.mult).then_inc(formed, 1)

                def link(ins, it, g, i):
                    ins.then_inc(chain, 1)
                    wait_in(dve, chain, it, LINKS, g * LINKS + i)

                def finish(it, g):
                    wait_in(dve, summed, it, T, (g + 1) * T)
                    for k in range(G1):
                        last = nc.vector.tensor_copy(zs[:, k:k + 1], acc_tile(g, G1, k)[:, F:FZ])
                    link(last, it, g, 1)
                    link(nc.vector.tensor_scalar(em, zs, 0.0, None, ALU.is_le), it, g, 2)
                    link(nc.vector.tensor_scalar(zs, zs, SMALL, None, ALU.max), it, g, 3)
                    link(nc.vector.reciprocal(zs, zs), it, g, 4)
                    dve.wait_ge(res_loaded, it * 32 + (g + 1) * 16)
                    for k in range(G1):
                        cols = slice(k * F, (k + 1) * F)
                        last = nc.vector.scalar_tensor_tensor(xr[:, cols], mean_row[:], em[:, k:k + 1], xr[:, cols],
                                                              ALU.mult, ALU.add)
                    link(last, it, g, 5)
                    if g >= 1:
                        dve.wait_ge(stored, it * 32 + g * 16)
                    for k in range(G1):
                        cols = slice(k * F, (k + 1) * F)
                        last = nc.vector.scalar_tensor_tensor(xo[:, cols], acc_tile(g, G1, k)[:, 0:F], zs[:, k:k + 1],
                                                              xr[:, cols], ALU.mult, ALU.add)
                    last.then_inc(acc_read, 1)

                def group(it, g):
                    if g == 1:
                        dve.wait_ge(r_loaded[2], 16)
                    for j in range(T):
                        form(it, g, j)
                        if g == 0 and j % (T // FOLDS) == 0 and j < T - T // FOLDS:
                            fold(h_folded, j // (T // FOLDS) + 1)
                        if j == 3 and g >= 1:
                            finish(it, g - 1)

                fold(h_folded, 0)
                for i in range(2):
                    dve.wait_ge(r_loaded[i], 16)
                groups_of(dve, NG1, group)
                finish(0, NG1 - 1)

            return sync_rows, scalar_rows, tensor_rows, vector_rows

        def run_paths(layer, fast, general):
            def unless_flagged(eng, which):
                flagged = eng.value_load(path[0:1, layer:layer + 1], min_val=0, max_val=1)
                with eng.If(flagged < 1):
                    fast[which](eng)

            def if_flagged(eng, which):
                flagged = eng.value_load(path[0:1, layer:layer + 1], min_val=0, max_val=1)
                with eng.If(flagged > 0):
                    general[which](eng)

            for choose in (unless_flagged, if_flagged):
                if choose is if_flagged and layer == 0:
                    weigh_risk()
                with nc.Block() as block:
                    @block.sync
                    def _(sp):
                        choose(sp, 0)

                    @block.scalar
                    def _(act):
                        choose(act, 1)

                    @block.tensor
                    def _(pe):
                        choose(pe, 2)

                    @block.vector
                    def _(dve):
                        choose(dve, 3)

        constants()
        for layer, x_in, W_in, a_in, x_to in ((0, x, W0, a0, x_mid), (1, x_mid, W1, a1, out)):
            prepare(layer, x_in, W_in, a_in)
            run_paths(layer, fast_path_0(x_in, x_to) if layer == 0 else fast_path_1(x_in, x_to),
                      general_path(layer, x_in, x_to))


_INS = ['x', 'adj', 'L0_gnn_W', 'L0_gnn_a', 'L1_gnn_W', 'L1_gnn_a']
_OUTS = [((8192, 128), 'float32')]


def kernel(**inputs):
    import numpy as _np
    import concourse.bacc as _bacc
    from concourse import mybir as _mybir
    from concourse.bass_utils import run_bass_kernel_spmd as _run

    nc = _bacc.Bacc("TRN2", target_bir_lowering=False, num_devices=1)
    arrays, args = {}, []
    for name in _INS:
        a = _np.ascontiguousarray(inputs[name])
        arrays[f"in_{name}_dram"] = a
        args.append(nc.dram_tensor(f"in_{name}_dram", a.shape, _mybir.dt.from_np(a.dtype), kind="ExternalInput").ap())
    for i, (shape, dtype) in enumerate(_OUTS):
        dt = _mybir.dt.from_np(_np.dtype(dtype))
        args.append(nc.dram_tensor(f"out_{i}_dram", shape, dt, kind="ExternalOutput").ap())
    kernel_program(nc, *args)
    r = _run(nc, [arrays], core_ids=[0])
    got = tuple(r.results[0][f"out_{i}_dram"] for i in range(len(_OUTS)))
    return got[0]
```
